# Optimizing a Trainium2 kernel written in Bass

```python
import numpy as np
import jax
import jax.numpy as jnp

def _softmax(x, axis=-1):
    return jax.nn.softmax(x, axis=axis)

def _gelu(x):
    return jax.nn.gelu(x, approximate=True)

def _silu(x):
    return jax.nn.silu(x)

def _sigmoid(x):
    return jax.nn.sigmoid(x)

def _layernorm(x, axis=-1, eps=1e-05):
    m = jnp.mean(x, axis=axis, keepdims=True)
    v = jnp.var(x, axis=axis, keepdims=True)
    return (x - m) / jnp.sqrt(v + eps)

def _scatter_add(tgt, idx, src, axis=0):
    return tgt.at[idx].add(src)

def _segment_sum(src, seg, n):
    return jax.ops.segment_sum(src, seg, n)
kernel_name = 'mk_adaln_ffn_d2_seqx_r8_c16988'

def setup_inputs(seed: int=0):
    np.random.seed(seed)
    _w = jnp.asarray

    def _rec_inputs():
        import jax
        import jax.numpy as jnp
        _rk = jax.random.key(seed)
        x = -7.109e-05 + 0.9999 * jax.random.normal(jax.random.fold_in(_rk, 1), (32, 32, 512), jnp.float32)
        _lenS = 32 - jax.random.randint(jax.random.fold_in(_rk, 7), (32,), 0, max(1, 32 // 4) + 1, jnp.int32)
        _lenS2 = 32 - jax.random.randint(jax.random.fold_in(_rk, 8), (32,), 0, max(1, 32 // 4) + 1, jnp.int32)
        itok_B_0_15 = jax.random.randint(jax.random.fold_in(_rk, 11), (32,), 0, 16, jnp.int32)
        itok_B_8_3872 = jax.random.randint(jax.random.fold_in(_rk, 12), (32,), 8, 3873, jnp.int32)
        return (x, itok_B_0_15, itok_B_8_3872)
    x, itok_B_0_15, itok_B_8_3872 = _rec_inputs()

    def _L0_cond_setup():
        import jax, jax.numpy as jnp
        import numpy as np
        NUM_CONDITIONS = 16
        IN_CH = 32
        OUT_CH = 32
        B = 64
        T = 512
        key = jax.random.key(seed)
        k_x, k_w, k_c = jax.random.split(key, 3)
        x = jax.random.normal(k_x, (B, IN_CH, T), dtype=jnp.float32)
        bound = float(np.sqrt(6.0 / IN_CH))
        weights = jax.random.uniform(k_w, (NUM_CONDITIONS, IN_CH, OUT_CH), dtype=jnp.float32, minval=-bound, maxval=bound)
        condition = jax.random.randint(k_c, (B,), 0, NUM_CONDITIONS, dtype=jnp.int64)
        return {'x': x, 'weights': weights, 'condition': condition}
    _L0_cond_all = _L0_cond_setup()
    _L0_cond_in = {k: v for k, v in _L0_cond_all.items() if k in ('weights',)}
    del _L0_cond_all

    def _L0_ffn_setup():
        import jax, jax.numpy as jnp
        import numpy as np
        DIM = 512
        INTER = 128
        E = 16
        GROUPS = 4
        LIM = 2
        K = 2
        SHARED_INTER = 2 * INTER
        SCALE = 1.0
        key = jax.random.key(seed)
        ks = jax.random.split(key, 16)

        def n(k, shape, s=0.02):
            return jax.random.normal(k, shape, jnp.float32) * s
        return {'x': jax.random.normal(ks[0], (1, 256, DIM), jnp.float32), 'router_w': n(ks[1], (DIM, E)), 'router_b': n(ks[2], (E,)), 'router_bias': n(ks[3], (E,), 1.0), 'ew1': n(ks[4], (E, DIM, INTER)), 'eb1': n(ks[5], (E, INTER)), 'ew2': n(ks[6], (E, DIM, INTER)), 'eb2': n(ks[7], (E, INTER)), 'ew3': n(ks[8], (E, INTER, DIM)), 'eb3': n(ks[9], (E, DIM)), 'sw1': n(ks[10], (DIM, SHARED_INTER)), 'sb1': n(ks[11], (SHARED_INTER,)), 'sw2': n(ks[12], (DIM, SHARED_INTER)), 'sb2': n(ks[13], (SHARED_INTER,)), 'sw3': n(ks[14], (SHARED_INTER, DIM)), 'sb3': n(ks[15], (DIM,))}
    _L0_ffn_all = _L0_ffn_setup()
    _L0_ffn_in = {k: v for k, v in _L0_ffn_all.items() if k in ('router_w', 'router_b', 'router_bias', 'ew1', 'eb1', 'ew2', 'eb2', 'ew3', 'eb3', 'sw1', 'sb1', 'sw2', 'sb2', 'sw3', 'sb3')}
    del _L0_ffn_all

    def _L1_cond_setup():
        import math
        import jax, jax.numpy as jnp
        import numpy as np
        H, N, B, L = (32, 64, 16, 512)
        DT_MIN, DT_MAX = (0.001, 0.1)

        def _get_kernel(log_dt, C, log_A_real, A_imag, length):
            Cc = C[..., 0] + 1j * C[..., 1]
            dt = jnp.exp(log_dt)
            A = -jnp.exp(log_A_real) + 1j * A_imag
            dtA = A * dt[:, None]
            P = dtA[:, :, None] * jnp.arange(length, dtype=jnp.float32)
            Cs = Cc * (jnp.exp(dtA) - 1.0) / A
            K = 2.0 * jnp.einsum('hn,hnl->hl', Cs, jnp.exp(P)).real
            return K
        key = jax.random.key(seed)
        ks = jax.random.split(key, 6)
        u = jax.random.normal(ks[0], (B, H, L), dtype=jnp.float32)
        length = jax.random.randint(ks[1], (B,), 0, L)
        log_dt = jax.random.uniform(ks[2], (H,), dtype=jnp.float32) * (math.log(DT_MAX) - math.log(DT_MIN)) + math.log(DT_MIN)
        C = jax.random.normal(ks[3], (H, N, 2), dtype=jnp.float32)
        log_A_real = jnp.log(0.5 * jnp.ones((H, N), dtype=jnp.float32))
        A_imag = math.pi * jnp.broadcast_to(jnp.arange(N, dtype=jnp.float32), (H, N))
        D = jax.random.normal(ks[4], (H,), dtype=jnp.float32)
        return {'u': u, 'length': length, 'log_dt': log_dt, 'C': C, 'log_A_real': log_A_real, 'A_imag': A_imag, 'D': D}
    _L1_cond_all = _L1_cond_setup()
    _L1_cond_in = {k: v for k, v in _L1_cond_all.items() if k in ('log_dt', 'C', 'log_A_real', 'A_imag', 'D')}
    del _L1_cond_all

    def _L1_ffn_setup():
        import jax, jax.numpy as jnp
        import numpy as np
        HID, INT, LAT, NE, K = (512, 1024, 256, 8, 2)
        LN_EPS = 1e-05

        def _layernorm(x, gamma, beta):
            mu = jnp.mean(x, axis=-1, keepdims=True)
            var = jnp.var(x, axis=-1, keepdims=True)
            return (x - mu) * jax.lax.rsqrt(var + LN_EPS) * gamma + beta
        key = jax.random.key(seed)
        ks = jax.random.split(key, 8)
        s = lambda d: 1.0 / np.sqrt(d)
        return {'hidden_states': jax.random.normal(ks[0], (4, 256, HID), jnp.float32), 'gate_w': jax.random.normal(ks[1], (HID, NE), jnp.float32) * s(HID), 'up_w': jax.random.normal(ks[2], (HID, INT), jnp.float32) * s(HID), 'down_w': jax.random.normal(ks[3], (INT, HID), jnp.float32) * s(INT), 'fc1_w': jax.random.normal(ks[4], (HID, LAT), jnp.float32) * s(HID), 'fc2_w': jax.random.normal(ks[5], (LAT, HID), jnp.float32) * s(LAT), 'expert_w': jax.random.normal(ks[6], (LAT, LAT), jnp.float32), 'ln_gamma': jnp.ones((HID,), jnp.float32), 'ln_beta': jnp.zeros((HID,), jnp.float32)}
    _L1_ffn_all = _L1_ffn_setup()
    _L1_ffn_in = {k: v for k, v in _L1_ffn_all.items() if k in ('gate_w', 'up_w', 'down_w', 'fc1_w', 'fc2_w', 'expert_w', 'ln_gamma', 'ln_beta')}
    del _L1_ffn_all
    return {'x': x, 'itok_B_0_15': itok_B_0_15, 'itok_B_8_3872': itok_B_8_3872, 'L0_cond_weights': _L0_cond_in['weights'], 'L0_ffn_router_w': _L0_ffn_in['router_w'], 'L0_ffn_router_b': _L0_ffn_in['router_b'], 'L0_ffn_router_bias': _L0_ffn_in['router_bias'], 'L0_ffn_ew1': _L0_ffn_in['ew1'], 'L0_ffn_eb1': _L0_ffn_in['eb1'], 'L0_ffn_ew2': _L0_ffn_in['ew2'], 'L0_ffn_eb2': _L0_ffn_in['eb2'], 'L0_ffn_ew3': _L0_ffn_in['ew3'], 'L0_ffn_eb3': _L0_ffn_in['eb3'], 'L0_ffn_sw1': _L0_ffn_in['sw1'], 'L0_ffn_sb1': _L0_ffn_in['sb1'], 'L0_ffn_sw2': _L0_ffn_in['sw2'], 'L0_ffn_sb2': _L0_ffn_in['sb2'], 'L0_ffn_sw3': _L0_ffn_in['sw3'], 'L0_ffn_sb3': _L0_ffn_in['sb3'], 'L1_cond_log_dt': _L1_cond_in['log_dt'], 'L1_cond_C': _L1_cond_in['C'], 'L1_cond_log_A_real': _L1_cond_in['log_A_real'], 'L1_cond_A_imag': _L1_cond_in['A_imag'], 'L1_cond_D': _L1_cond_in['D'], 'L1_ffn_gate_w': _L1_ffn_in['gate_w'], 'L1_ffn_up_w': _L1_ffn_in['up_w'], 'L1_ffn_down_w': _L1_ffn_in['down_w'], 'L1_ffn_fc1_w': _L1_ffn_in['fc1_w'], 'L1_ffn_fc2_w': _L1_ffn_in['fc2_w'], 'L1_ffn_expert_w': _L1_ffn_in['expert_w'], 'L1_ffn_ln_gamma': _L1_ffn_in['ln_gamma'], 'L1_ffn_ln_beta': _L1_ffn_in['ln_beta']}

def reference(x, itok_B_0_15, itok_B_8_3872, L0_cond_weights, L0_ffn_router_w, L0_ffn_router_b, L0_ffn_router_bias, L0_ffn_ew1, L0_ffn_eb1, L0_ffn_ew2, L0_ffn_eb2, L0_ffn_ew3, L0_ffn_eb3, L0_ffn_sw1, L0_ffn_sb1, L0_ffn_sw2, L0_ffn_sb2, L0_ffn_sw3, L0_ffn_sb3, L1_cond_log_dt, L1_cond_C, L1_cond_log_A_real, L1_cond_A_imag, L1_cond_D, L1_ffn_gate_w, L1_ffn_up_w, L1_ffn_down_w, L1_ffn_fc1_w, L1_ffn_fc2_w, L1_ffn_expert_w, L1_ffn_ln_gamma, L1_ffn_ln_beta):
    import jax
    import jax.numpy as jnp

    def _L0_cond_ref(x, weights, condition):
        import jax, jax.numpy as jnp
        import numpy as np
        NUM_CONDITIONS = 16
        IN_CH = 32
        OUT_CH = 32
        B = 64
        T = 512
        W = weights[condition]
        return jnp.einsum('bct,bcd->bdt', x, W)

    def _L0_ffn_ref(x, router_w, router_b, router_bias, ew1, eb1, ew2, eb2, ew3, eb3, sw1, sb1, sw2, sb2, sw3, sb3):
        import jax, jax.numpy as jnp
        import numpy as np
        DIM = 512
        INTER = 128
        E = 16
        GROUPS = 4
        LIM = 2
        K = 2
        SHARED_INTER = 2 * INTER
        SCALE = 1.0
        shape = x.shape
        xt = x.reshape(-1, DIM)
        T = xt.shape[0]
        logits = xt @ router_w + router_b
        scores = jax.nn.softmax(logits.astype(jnp.float32), axis=-1) + router_bias
        g = scores.reshape(T, GROUPS, E // GROUPS)
        _, gidx = jax.lax.top_k(g.max(axis=-1), LIM)
        keep = jnp.zeros((T, GROUPS), bool).at[jnp.arange(T)[:, None], gidx].set(True)
        masked = jnp.where(keep[:, :, None], g, -jnp.inf).reshape(T, E)
        _, idx = jax.lax.top_k(masked, K)
        vals = (jnp.take_along_axis(scores, idx, axis=1) * SCALE).astype(x.dtype)
        gate = jnp.zeros((T, E), x.dtype).at[jnp.arange(T)[:, None], idx].add(vals)

        def step(y, p):
            w1, b1, w2, b2, w3, b3, ge = p
            h = jax.nn.silu(xt @ w1 + b1) * (xt @ w2 + b2)
            return (y + ge[:, None] * (h @ w3 + b3), None)
        y, _ = jax.lax.scan(step, jnp.zeros_like(xt), (ew1, eb1, ew2, eb2, ew3, eb3, gate.T))
        z = jax.nn.silu(xt @ sw1 + sb1) * (xt @ sw2 + sb2) @ sw3 + sb3
        return (y + z).reshape(shape)

    def _L1_cond_ref(u, length, log_dt, C, log_A_real, A_imag, D):
        import math
        import jax, jax.numpy as jnp
        import numpy as np
        H, N, B, L = (32, 64, 16, 512)
        DT_MIN, DT_MAX = (0.001, 0.1)

        def _get_kernel(log_dt, C, log_A_real, A_imag, length):
            Cc = C[..., 0] + 1j * C[..., 1]
            dt = jnp.exp(log_dt)
            A = -jnp.exp(log_A_real) + 1j * A_imag
            dtA = A * dt[:, None]
            P = dtA[:, :, None] * jnp.arange(length, dtype=jnp.float32)
            Cs = Cc * (jnp.exp(dtA) - 1.0) / A
            K = 2.0 * jnp.einsum('hn,hnl->hl', Cs, jnp.exp(P)).real
            return K
        Bq, Hq, Lq = u.shape
        mask = (jnp.arange(Lq) < length[:, None]).astype(u.dtype)
        u_m = u * mask[:, None, :]
        kernel = _get_kernel(log_dt, C, log_A_real, A_imag, Lq)
        n = 2 * Lq
        k_f = jnp.fft.rfft(kernel, n=n)
        u_f = jnp.fft.rfft(u_m, n=n)
        y = jnp.fft.irfft(u_f * k_f, n=n)[..., :Lq]
        y = y + u_m * D[:, None]
        return y * mask[:, None, :]

    def _L1_ffn_ref(hidden_states, gate_w, up_w, down_w, fc1_w, fc2_w, expert_w, ln_gamma, ln_beta):
        import jax, jax.numpy as jnp
        import numpy as np
        HID, INT, LAT, NE, K = (512, 1024, 256, 8, 2)
        LN_EPS = 1e-05

        def _layernorm(x, gamma, beta):
            mu = jnp.mean(x, axis=-1, keepdims=True)
            var = jnp.var(x, axis=-1, keepdims=True)
            return (x - mu) * jax.lax.rsqrt(var + LN_EPS) * gamma + beta
        logits = jnp.einsum('bsh,he->bse', hidden_states, gate_w)
        routing_weights, selected_experts = jax.lax.top_k(logits, K)
        h = jax.nn.relu(jnp.einsum('bsh,hi->bsi', hidden_states, up_w)) ** 2
        shared_out = jnp.einsum('bsi,ih->bsh', h, down_w)
        x_latent = jnp.einsum('bsh,hl->bsl', hidden_states, fc1_w)
        expert_out = jnp.einsum('bsl,lm->bsm', x_latent, expert_w)
        moe_out = expert_out * jnp.sum(routing_weights, axis=-1, keepdims=True)
        routed_out = jnp.einsum('bsl,lh->bsh', moe_out, fc2_w)
        return _layernorm(shared_out + routed_out, ln_gamma, ln_beta)
    x = x + _L0_ffn_ref(_L0_cond_ref(x, L0_cond_weights, itok_B_0_15), L0_ffn_router_w, L0_ffn_router_b, L0_ffn_router_bias, L0_ffn_ew1, L0_ffn_eb1, L0_ffn_ew2, L0_ffn_eb2, L0_ffn_ew3, L0_ffn_eb3, L0_ffn_sw1, L0_ffn_sb1, L0_ffn_sw2, L0_ffn_sb2, L0_ffn_sw3, L0_ffn_sb3)
    x = x + _L1_ffn_ref(_L1_cond_ref(x, itok_B_8_3872, L1_cond_log_dt, L1_cond_C, L1_cond_log_A_real, L1_cond_A_imag, L1_cond_D), L1_ffn_gate_w, L1_ffn_up_w, L1_ffn_down_w, L1_ffn_fc1_w, L1_ffn_fc2_w, L1_ffn_expert_w, L1_ffn_ln_gamma, L1_ffn_ln_beta)
    return x

_drawn_inputs = setup_inputs


def setup_inputs(seed=0):
    import zlib

    import numpy as np

    out = dict(_drawn_inputs(seed))
    spreads = {'L1_cond_log_A_real': (-0.6931471824645996, 0.2),
     'L1_ffn_ln_gamma': (1.0, 0.2),
     'L1_ffn_ln_beta': (0.0, 0.1)}
    factors = {'L0_ffn_router_w': 4.311,
     'L0_ffn_router_b': 37.212,
     'L0_ffn_eb1': 8.0,
     'L0_ffn_eb2': 8.0,
     'L0_ffn_sb1': 8.0,
     'L0_ffn_sb2': 8.0,
     'L0_ffn_sb3': 2.712}
    for name, (base, spread) in spreads.items():
        noise = np.random.default_rng([zlib.crc32(name.encode()), seed]).standard_normal(out[name].shape)
        drawn = base * np.exp(spread * noise) if base else spread * noise
        out[name] = jnp.asarray(drawn.astype(out[name].dtype))
    for name, factor in factors.items():
        out[name] = (out[name] * factor).astype(out[name].dtype)
    return out
```

```python
import math
from contextlib import ExitStack

import concourse.bass as bass
import numpy as np
from concourse import mybir

F32 = mybir.dt.float32
F32R = mybir.dt.float32r
I32 = mybir.dt.int32
U32 = mybir.dt.uint32
ALU = mybir.AluOpType
ACT = mybir.ActivationFunctionType
AX = mybir.AxisListType

P = 128
MAGIC = 1.5 * 2.0 ** 23
BIG = 3.0e38
LN_EPS = 1e-5
PI_1 = 6.28125
PI_2 = float(np.float32(np.floor((2 * math.pi - PI_1) * 2 ** 21) / 2 ** 21))
PI_3 = float(np.float32(2 * math.pi - PI_1 - PI_2))
PI_SAFE = 3.1415925


def adaln_ffn_program(nc, x, cond, length, cond_w, router_w, router_b, router_bias, ew1, eb1, ew2, eb2, ew3, eb3,
                      sw1, sb1, sw2, sb2, sw3, sb3, log_dt, c_param, log_a_real, a_imag, d_param,
                      gate_w, up_w, down_w, fc1_w, fc2_w, expert_w, ln_gamma, ln_beta, out):
    B, C, T = x.shape
    N = B * C
    NT = N // P
    KC = T // P
    BT = P // C
    HALF = N // 2
    TH = NT // 2
    E, _, INTER = ew1.shape
    SH = sw1.shape[1] // INTER
    G = SH + E
    NG = 4
    INT1 = up_w.shape[1]
    JC = INT1 // P
    LAT = fc1_w.shape[1]
    LC = LAT // P
    NE1 = gate_w.shape[1]
    HN = a_imag.shape[1]
    LI = 16
    LJ = T // LI
    NL = 2 * LI + LJ + 2
    PAD = P + T
    TS = 24
    WCOLS = 2 * KC * INTER + T
    ITS = G // 2
    assert INTER == P and SH == 2 and 2 * HN == P and G % 2 == 0

    kpad = nc.dram_tensor("kpad", [C, PAD], F32).ap()

    base = 16512
    cursor = [base]

    def region(size):
        at = cursor[0]
        cursor[0] += size
        return [at]

    def at(reg, name, shape, dt=F32):
        width = int(np.prod(shape[1:])) * 4
        t = nc.alloc_sbuf_tensor_at(name, shape, dt, offset=reg[0])
        reg[0] += (width + 31) // 32 * 32
        return t

    main = region(3 * NT * T * 4)
    acc = at(main, "acc", [P, NT, T])
    ah = at(main, "ah", [P, KC, N], F32R)
    al = at(main, "al", [P, KC, N], F32R)
    toep_at = cursor[0]
    toep_reg = region(TS * T * 4)
    toep = at(toep_reg, "toep", [P, TS, T])
    exp_at = cursor[0]
    exp_reg = region((6 * WCOLS + 8 * HALF) * 4)
    wraw = at(exp_reg, "wraw", [P, 2, WCOLS])
    whi = at(exp_reg, "whi", [P, 2, WCOLS], F32R)
    wlo = at(exp_reg, "wlo", [P, 2, WCOLS], F32R)
    silu = at(exp_reg, "silu", [P, 2, HALF])
    hid = at(exp_reg, "hid", [P, 2, HALF])
    hidh = at(exp_reg, "hidh", [P, 2, HALF], F32R)
    hidl = at(exp_reg, "hidl", [P, 2, HALF], F32R)
    raw_at = cursor[0]
    raw_reg = region(2 * KC * INT1 * 4)
    upraw = at(raw_reg, "upraw", [P, KC, INT1])
    dnraw = at(raw_reg, "dnraw", [P, JC, T])
    r = [toep_at]
    phase = at(r, "phase", [P, C, NL])
    decay = at(r, "decay", [P, C, NL])
    turns = at(r, "turns", [P, C, NL])
    term = at(r, "term", [P, C, NL])
    angle = at(r, "angle", [P, C, NL])
    lhs_k = at(r, "lhs_k", [P, C, LI])
    r = [toep_at]
    tmp_k = at(r, "tmp_k", [P, C, LI])
    r = [toep_at]
    kout = at(r, "kout", [LI, C, LJ])
    r = [toep_at]
    dnh = at(r, "dnh", [P, JC, T], F32R)
    dnl = at(r, "dnl", [P, JC, T], F32R)
    r = [exp_at + 2 * KC * INT1 * 4]
    m2h = at(r, "m2h", [P, LC, T], F32R)
    m2l = at(r, "m2l", [P, LC, T], F32R)
    fch = at(r, "fch", [P, KC, LAT], F32R)
    fcl = at(r, "fcl", [P, KC, LAT], F32R)
    r = [exp_at]
    uph = at(r, "uph", [P, KC, INT1], F32R)
    upl = at(r, "upl", [P, KC, INT1], F32R)
    u_t = at(r, "u_t", [P, C, KC, B])
    r = [raw_at]
    wbd = at(r, "wbd", [P, NT, P])
    wsel = at(r, "wsel", [P, NT, C])
    ewraw = at(r, "ewraw", [P, LC, LAT])
    bstage = at(r, "bstage", [G, 2, P])
    sstage = at(r, "sstage", [C, 4, P])
    cstage = at(r, "cstage", [C, HN, 2])
    r = [raw_at]
    rel = at(r, "rel", [P, 2, HALF])
    sqh = at(r, "sqh", [P, 2, HALF], F32R)
    sql = at(r, "sql", [P, 2, HALF], F32R)
    r = [raw_at + KC * INT1 * 4]
    lath = at(r, "lath", [P, LC, HALF], F32R)
    latl = at(r, "latl", [P, LC, HALF], F32R)
    routed = at(r, "routed", [P, 2, T])
    osum = at(r, "osum", [P, 2, T])
    r = [exp_at + 2 * KC * INT1 * 4 + N * KC * 4]
    ycv = at(r, "ycv", [P, 2, 4, P])
    r = [exp_at + 2 * KC * INT1 * 4 + N * KC * 4]
    arev = at(r, "arev", [P, 2, T])
    r = [exp_at + 2 * KC * INT1 * 4 + N * KC * 4]
    sq = at(r, "sq", [P, 2, HALF])

    small = [cursor[0]]
    ident = at(small, "ident", [P, P])
    r = list(small)
    gt = at(small, "gt", [G, N])
    gam = at(r, "gam", [P, T])
    bet = at(r, "bet", [P, T])
    b3m = at(small, "b3m", [G, T])
    fcraw = at(small, "fcraw", [P, KC, LAT])
    fc2raw = at(small, "fc2raw", [P, LC, T])
    ewt = at(small, "ewt", [P, LC, LAT])
    rwraw = at(small, "rwraw", [P, KC, E])
    rwh = at(small, "rwh", [P, KC, E], F32R)
    rwl = at(small, "rwl", [P, KC, E], F32R)
    gwraw = at(small, "gwraw", [P, KC, NE1])
    gwh = at(small, "gwh", [P, KC, NE1], F32R)
    gwl = at(small, "gwl", [P, KC, NE1], F32R)
    rb = at(small, "rb", [P, 2, E])
    b12 = at(small, "b12", [P, 2, G])
    b1cur = at(small, "b1cur", [P, 2])
    gates = at(small, "gates", [P, G, NT])
    sc = at(small, "sc", [P, NT, E])
    w1t = at(small, "w1t", [P, NT, E])
    w2t = at(small, "w2t", [P, NT, E])
    oh1 = at(small, "oh1", [P, NT, E])
    oh2 = at(small, "oh2", [P, NT, E])
    gm = at(small, "gm", [P, NT, NG])
    keep = at(small, "keep", [P, NT, NG])
    desc = at(small, "desc", [P, E])
    desci = at(small, "desci", [P, E], I32)
    cidx = at(small, "cidx", [P, NT], I32)
    condb = at(small, "condb", [P, B], I32)
    cpart = at(small, "cpart", [P, NT], I32)
    red = at(small, "red", [P, 2, NT])
    leni = at(small, "leni", [P, B], I32)
    lenf = at(small, "lenf", [P, B])
    tpos = at(small, "tpos", [P, 2, KC])
    tposi = at(small, "tposi", [P, 2, KC], I32)
    mask = at(small, "mask", [P, 2, KC, B])
    spar = at(small, "spar", [P, 4, C])
    sdt = at(small, "sdt", [P, C])
    sw = at(small, "sw", [P, 14, C])
    dimh = at(small, "dimh", [P, C], F32R)
    lvals = at(small, "lvals", [P, NL])
    lvali = at(small, "lvali", [P, NL], I32)
    shq = at(small, "shq", [P, NL])
    shr = at(small, "shr", [P, NL])
    drow = at(small, "drow", [1, C])
    zrow = at(small, "zrow", [C, P])
    top8 = at(small, "top8", [P, NT, 8])
    rsc = at(small, "rsc", [P, NT])
    stats = at(small, "stats", [P, NT, 6])
    mv = at(small, "mv", [P, NT, 2])
    std = at(small, "std", [P, NT])
    rstd = at(small, "rstd", [P, NT])
    nmr = at(small, "nmr", [P, NT])
    epst = at(small, "epst", [P, 1])
    assert small[0] <= nc.sbuf_usable_end, (small, nc.sbuf_usable_end)

    bank = [nc.alloc_psum_tensor(f"bank{i}", [P, 512], F32) for i in range(8)]

    ctx = ExitStack()

    def sem(name):
        return ctx.enter_context(nc.semaphore(name))

    x_in = [sem(f"x_in{i}") for i in range(4)]
    cond_in, wsel_in, bias_in, router_in, s4_in, s4b_in, len_in = (sem(s) for s in (
        "cond_in", "wsel_in", "bias_in", "router_in", "s4_in", "s4b_in", "len_in"))
    raw_in = [sem("raw_in0"), sem("raw_in1")]
    l1_in, big_in, ln_in, kz_in, kpad_in = (sem(s) for s in ("l1_in", "big_in", "ln_in", "kz_in", "kpad_in"))
    toep_in = [sem("toep_in0"), sem("toep_in1")]
    out_sem = sem("out_sem")
    ident_ok, pool_step, vec_step, act_step = sem("ident_ok"), sem("pool_step"), sem("vec_step"), sem("act_step")
    cidx_ok, wbd_ok, mix_done, ah_ok, al_ok = (sem(s) for s in ("cidx_ok", "wbd_ok", "mix_done", "ah_ok", "al_ok"))
    rw_ok, gw_ok, tr_done, spar_ok, lg_done = (sem(s) for s in ("rw_ok", "gw_ok", "tr_done", "spar_ok", "lg_done"))
    whi_ok = [sem("whi_ok0"), sem("whi_ok1")]
    wlo_ok = [sem("wlo_ok0"), sem("wlo_ok1")]
    a_done, c_done, y_done = sem("a_done"), sem("c_done"), sem("y_done")
    silu_ok, hid_ok, hidh_ok, hidl_ok, y_added = (sem(s) for s in ("silu_ok", "hid_ok", "hidh_ok", "hidl_ok", "y_added"))
    soft_in, soft_out, gates_ok, gt_done, gt_ok, b3_done, b3_added = (sem(s) for s in (
        "soft_in", "soft_out", "gates_ok", "gt_done", "gt_ok", "b3_done", "b3_added"))
    exps_ok, angle_ok, trig_ok, lhs_ok, k_done, kout_ok, mask_ok = (sem(s) for s in (
        "exps_ok", "angle_ok", "trig_ok", "lhs_ok", "k_done", "kout_ok", "mask_ok"))
    cpart_ok, desc_ok, lenf_ok, stage_ok, b3z_ok = (sem(s) for s in (
        "cpart_ok", "desc_ok", "lenf_ok", "stage_ok", "b3z_ok"))
    dimh_ok, den_ok, rden_ok, dim_ok, kd_ok = (sem(s) for s in ("dimh_ok", "den_ok", "rden_ok", "dim_ok", "kd_ok"))
    arev_ok, b1cur_ok, b12_ok, ewt_ok = sem("arev_ok"), sem("b1cur_ok"), sem("b12_ok"), sem("ewt_ok")
    xt_done, u_ok, conv_done, y_ok, yh_ok, yl_ok, uph_ok, upl_ok = (sem(s) for s in (
        "xt_done", "u_ok", "conv_done", "y_ok", "yh_ok", "yl_ok", "uph_ok", "upl_ok"))
    dnh_ok, dnl_ok, fch_ok, fcl_ok, m2_done, m2h_ok, m2l_ok, resid_ok = (sem(s) for s in (
        "dnh_ok", "dnl_ok", "fch_ok", "fcl_ok", "m2_done", "m2h_ok", "m2l_ok", "resid_ok"))
    lg1_done, top_ok, rsc_ok, up_done, rel_ok, sq_ok, sqh_ok, sql_ok = (sem(s) for s in (
        "lg1_done", "top_ok", "rsc_ok", "up_done", "rel_ok", "sq_ok", "sqh_ok", "sql_ok"))
    dn_done, lat_done, lath_ok, latl_ok, rt_done, rt_ok, osum_ok, var_ok = (sem(s) for s in (
        "dn_done", "lat_done", "lath_ok", "latl_ok", "rt_done", "rt_ok", "osum_ok", "var_ok"))
    std_ok, nmr_ok, norm_ok, fin_ok = (sem(s) for s in ("std_ok", "nmr_ok", "norm_ok", "fin_ok"))

    def wait(eng, s, v):
        if isinstance(v, int) and v <= 0:
            return
        eng.wait_ge(s, v)

    def f(ap):
        return ap.bitcast(F32)

    xf = x.rearrange("b c t -> (b c) t")
    of = out.rearrange("b c t -> (b c) t")
    FULL_LOOPS = ((1, 4), (4, 6), (6, ITS - 1))
    LAST = ITS - 1

    def split3(pe, dst, lhs, rhs, n_k, **kw):
        for k in range(n_k):
            (lh, ll), (rh, rl) = lhs(k), rhs(k)
            pe.matmul(dst, lh, rh, start=(k == 0), stop=False, **kw)
            pe.matmul(dst, lh, rl, start=False, stop=False, **kw)
            mm = pe.matmul(dst, ll, rh, start=False, stop=(k == n_k - 1), **kw)
        return mm

    block = ctx.enter_context(nc.Block())

    @block.sync
    def _(sp):
        def load_expert(par, w1, w2, w3):
            sp.dma_start(wraw[:, par, 0:KC * P].rearrange("p (k m) -> p k m", k=KC), w1).then_inc(raw_in[par], 16)
            sp.dma_start(wraw[:, par, KC * P:2 * KC * P].rearrange("p (k m) -> p k m", k=KC), w2)\
                .then_inc(raw_in[par], 16)
            sp.dma_start(wraw[:, par, 2 * KC * P:], w3).then_inc(raw_in[par], 16)

        for j in range(4):
            sp.dma_start(acc[:, 2 * j:2 * j + 2, :],
                         xf[2 * j * P:(2 * j + 2) * P, :].rearrange("(i p) t -> p i t", p=P)).then_inc(x_in[j], 16)
        for par in range(2):
            load_expert(par, sw1[:, par * P:(par + 1) * P].rearrange("(k p) m -> p k m", p=P),
                        sw2[:, par * P:(par + 1) * P].rearrange("(k p) m -> p k m", p=P),
                        sw3[par * P:(par + 1) * P, :])

        def prefetch(it):
            for par in range(2):
                wait(sp, whi_ok[par], it + 1)
                wait(sp, wlo_ok[par], it + 1)
                e = it * 2 + par
                load_expert(par, ew1[bass.ds(e, 1)].rearrange("o (k p) m -> p (o k) m", p=P),
                            ew2[bass.ds(e, 1)].rearrange("o (k p) m -> p (o k) m", p=P),
                            ew3[bass.ds(e, 1)].rearrange("o p n -> (o p) n"))

        prefetch(0)
        with sp.Fori(1, LAST) as it:
            prefetch(it)
        for i in range(NT):
            wait(sp, fin_ok, i + 1)
            sp.dma_start(of[i * P:(i + 1) * P, :], acc[:, i, :]).then_inc(out_sem, 16)
        wait(sp, out_sem, 16 * NT)

    @block.gpsimd
    def _(pool):
        steps = [0]

        def link(ins):
            steps[0] += 1
            ins.then_inc(pool_step, 1)
            pool.wait_ge(pool_step, steps[0])

        pool.iota(cpart[:, :], pattern=[[0, NT]], base=0, channel_multiplier=1).then_inc(cpart_ok, 1)
        wait(pool, cidx_ok, 1)
        for i in range(NT):
            pool.indirect_dma_start(wsel[:, i, :], None, cond_w.rearrange("k c d -> (k c) d"),
                                    bass.IndirectOffsetOnAxis(ap=cidx[:, i:i + 1].bitcast(U32), axis=0))\
                .then_inc(wsel_in, 16)
        link(pool.memset(ident[:, :], 0.0))
        pool.affine_select(out=ident[:, :], in_=ident[:, :], compare_op=ALU.not_equal, fill=1.0, base=0,
                           pattern=[[-1, P]], channel_multiplier=1).then_inc(ident_ok, 1)
        link(pool.iota(tposi[:, 0, :], pattern=[[P, KC]], base=0, channel_multiplier=1))
        link(pool.iota(tposi[:, 1, :], pattern=[[P, KC]], base=P - 1, channel_multiplier=-1))
        link(pool.tensor_copy(tpos[:, :, :], tposi[:, :, :]))
        link(pool.iota(desci[:, :], pattern=[[-1, E]], base=E, channel_multiplier=0))
        pool.tensor_copy(desc[:, :], desci[:, :]).then_inc(desc_ok, 1)
        link(pool.iota(lvali[:, 0:2 * LI], pattern=[[0, 2], [LJ, LI]], base=0, channel_multiplier=0))
        link(pool.iota(lvali[:, 2 * LI:2 * LI + LJ], pattern=[[1, LJ]], base=0, channel_multiplier=0))
        link(pool.iota(lvali[:, NL - 2:NL], pattern=[[0, 2]], base=1, channel_multiplier=0))
        link(pool.tensor_copy(lvals[:, :], lvali[:, :]))
        for row in range(2):
            ps = slice(row * HN, (row + 1) * HN)
            for a, b, v in ((0, LI, row), (LI, 2 * LI, row + 1), (2 * LI, 2 * LI + LJ, 1 - row),
                            (NL - 2, NL - 1, 0), (NL - 1, NL, 1)):
                link(pool.memset(shq[ps, a:b], v / 4))
        link(pool.tensor_scalar(shr[:, :], shq[:, :], 2 * math.pi, None, ALU.mult))
        link(pool.memset(epst[:, :], LN_EPS))
        pool.wait_ge(len_in, 16)
        pool.tensor_copy(lenf[:, :], leni[:, :]).then_inc(lenf_ok, 1)
        link(pool.memset(zrow[:, :], 0.0))
        pool.dma_start(kpad[:, 0:P], zrow[:, :]).then_inc(kz_in, 16)

        pool.wait_ge(s4_in, 64)
        link(pool.tensor_copy(sstage[:, 2, 0:HN], cstage[:, :, 0]))
        link(pool.tensor_copy(sstage[:, 2, HN:P], cstage[:, :, 0]))
        link(pool.tensor_copy(sstage[:, 3, 0:HN], cstage[:, :, 1]))
        pool.tensor_copy(sstage[:, 3, HN:P], cstage[:, :, 1]).then_inc(stage_ok, 1)
        EA, DT, DRE, DIM, DLO, DEN, RDEN, NR, QR, QI, X1, X2, CR2, CI2 = range(14)
        w = [sw[:, k, :] for k in range(14)]
        pool.wait_ge(exps_ok, 2)
        link(pool.tensor_tensor(w[DRE], w[EA], w[DT], ALU.mult))
        link(pool.tensor_tensor(w[DIM], spar[:, 1, :], w[DT], ALU.mult))
        link(pool.tensor_tensor(w[X1], w[EA], w[EA], ALU.mult))
        link(pool.tensor_tensor(w[X2], spar[:, 1, :], spar[:, 1, :], ALU.mult))
        link(pool.tensor_tensor(w[DEN], w[X1], w[X2], ALU.add))
        pool.tensor_copy(w[X1], w[DIM]).then_inc(dim_ok, 1)
        pool.wait_ge(dimh_ok, 1)
        link(pool.tensor_tensor(w[DLO], w[DIM], f(dimh[:, :]), ALU.subtract))

        def cols(ap):
            return ap.unsqueeze(2).broadcast_to([P, C, NL])

        def heads(ap):
            return ap.unsqueeze(1).broadcast_to([P, C, NL])

        link(pool.tensor_tensor(decay[:, :, :], cols(w[DRE]), heads(lvals[:, :]), ALU.mult))
        link(pool.tensor_tensor(phase[:, :, :], cols(w[DIM]), heads(lvals[:, :]), ALU.mult))
        link(pool.tensor_scalar(phase[:, :, :], phase[:, :, :], 1 / (2 * math.pi), None, ALU.mult))
        link(pool.tensor_tensor(turns[:, :, :], phase[:, :, :], heads(shq[:, :]), ALU.add))
        link(pool.tensor_scalar(turns[:, :, :], turns[:, :, :], MAGIC, None, ALU.add))
        link(pool.tensor_scalar(turns[:, :, :], turns[:, :, :], -MAGIC, None, ALU.add))
        link(pool.tensor_tensor(angle[:, :, :], cols(f(dimh[:, :])), heads(lvals[:, :]), ALU.mult))
        link(pool.tensor_scalar(term[:, :, :], turns[:, :, :], PI_1, None, ALU.mult))
        link(pool.tensor_tensor(angle[:, :, :], angle[:, :, :], term[:, :, :], ALU.subtract))
        link(pool.tensor_scalar(term[:, :, :], turns[:, :, :], PI_2, None, ALU.mult))
        link(pool.tensor_tensor(angle[:, :, :], angle[:, :, :], term[:, :, :], ALU.subtract))
        link(pool.tensor_tensor(phase[:, :, :], cols(w[DLO]), heads(lvals[:, :]), ALU.mult))
        link(pool.tensor_scalar(term[:, :, :], turns[:, :, :], PI_3, None, ALU.mult))
        link(pool.tensor_tensor(phase[:, :, :], phase[:, :, :], term[:, :, :], ALU.subtract))
        link(pool.tensor_tensor(phase[:, :, :], phase[:, :, :], heads(shr[:, :]), ALU.add))
        link(pool.tensor_tensor(angle[:, :, :], angle[:, :, :], phase[:, :, :], ALU.add))
        pool.tensor_scalar(angle[:, :, :], angle[:, :, :], PI_SAFE, -PI_SAFE, ALU.min, ALU.max).then_inc(angle_ok, 1)

        wait(pool, b3_done, NT)
        for dst, src in ((gam, ln_gamma), (bet, ln_beta)):
            pool.dma_start(dst[:, :], bass.AP(tensor=src.tensor, offset=0, ap=[[0, P], [1, T]])).then_inc(ln_in, 16)
        wait(pool, mix_done, NT)
        wait(pool, tr_done, 3)
        pool.dma_start(upraw[:, :, :], up_w.rearrange("(k p) m -> p k m", p=P)).then_inc(big_in, 16)
        pool.dma_start(dnraw[:, :, :], down_w.rearrange("(j p) n -> p j n", p=P)).then_inc(big_in, 16)

        pool.wait_ge(trig_ok, 2)
        link(pool.tensor_tensor(term[:, :, :], decay[:, :, :], angle[:, :, :], ALU.mult))
        pool.wait_ge(rden_ok, 1)
        er, ei = term[:, :, NL - 1], term[:, :, NL - 2]
        link(pool.tensor_scalar(w[NR], er, -1.0, None, ALU.add))
        link(pool.tensor_tensor(w[X1], ei, spar[:, 1, :], ALU.mult))
        link(pool.tensor_tensor(w[X2], w[NR], w[EA], ALU.mult))
        link(pool.tensor_tensor(w[X1], w[X1], w[X2], ALU.subtract))
        link(pool.tensor_tensor(w[QR], w[X1], w[RDEN], ALU.mult))
        link(pool.tensor_tensor(w[X1], w[NR], spar[:, 1, :], ALU.mult))
        link(pool.tensor_tensor(w[X2], ei, w[EA], ALU.mult))
        link(pool.tensor_tensor(w[X1], w[X1], w[X2], ALU.add))
        link(pool.tensor_tensor(w[X1], w[X1], w[RDEN], ALU.mult))
        link(pool.tensor_scalar(w[QI], w[X1], -1.0, None, ALU.mult))
        for dst, a, b, op in ((CR2, QR, QI, ALU.subtract), (CI2, QI, QR, ALU.add)):
            link(pool.tensor_tensor(w[X1], spar[:, 2, :], w[a], ALU.mult))
            link(pool.tensor_tensor(w[X2], spar[:, 3, :], w[b], ALU.mult))
            link(pool.tensor_tensor(w[X1], w[X1], w[X2], op))
            link(pool.tensor_scalar(w[dst], w[X1], 2.0, None, ALU.mult))

        def ncols(ap):
            return ap.unsqueeze(2).broadcast_to([P, C, LI])

        link(pool.tensor_tensor(lhs_k[:, :, :], term[:, :, LI:2 * LI], ncols(w[CR2]), ALU.mult))
        link(pool.tensor_tensor(tmp_k[:, :, :], term[:, :, 0:LI], ncols(w[CI2]), ALU.mult))
        pool.tensor_tensor(lhs_k[:, :, :], lhs_k[:, :, :], tmp_k[:, :, :], ALU.subtract).then_inc(lhs_ok, 1)

        pool.wait_ge(kout_ok, 2)
        pool.tensor_tensor(kout[0:1, :, 0], kout[0:1, :, 0], drow[:, :], ALU.add).then_inc(kd_ok, 1)
        pool.wait_ge(kd_ok, 1)
        pool.dma_start(kpad[:, P:PAD].rearrange("h (i j) -> i h j", i=LI), kout[:, :, :]).then_inc(kpad_in, 16)
        pool.wait_ge(kz_in, 16)
        pool.wait_ge(kpad_in, 16)

        def toeplitz(h0, n):
            return bass.AP(tensor=kpad.tensor, offset=h0 * PAD + 1, ap=[[1, P], [PAD, n], [1, T]])

        for h in range(0, TS, TS // 2):
            pool.dma_start(toep[:, h:h + TS // 2, :], toeplitz(h, TS // 2)).then_inc(toep_in[0], 16)
        pool.wait_ge(conv_done, C - TS)
        pool.dma_start(toep[:, 0:C - TS, :], toeplitz(TS, C - TS)).then_inc(toep_in[1], 16)
        pool.wait_ge(uph_ok, KC)
        pool.wait_ge(ln_in, 32)
        for k in range(KC):
            pool.tensor_tensor(upl[:, k, :], upraw[:, k, :], f(uph[:, k, :]), ALU.subtract).then_inc(upl_ok, 1)
        for i in range(NT):
            pool.wait_ge(xt_done, i + 1)
            pool.tensor_tensor(acc[:, i, :], acc[:, i, :], bet[:, :], ALU.add).then_inc(resid_ok, 1)
        for j in range(JC):
            pool.wait_ge(dnh_ok, j + 1)
            pool.tensor_tensor(dnl[:, j, :], dnraw[:, j, :], f(dnh[:, j, :]), ALU.subtract).then_inc(dnl_ok, 1)
        pool.wait_ge(fch_ok, 1)
        pool.tensor_tensor(fcl[:, :, :], fcraw[:, :, :], f(fch[:, :, :]), ALU.subtract).then_inc(fcl_ok, 1)

    @block.scalar
    def _(act):
        def bcast(src, n):
            return bass.AP(tensor=src.tensor, offset=0, ap=[[0, P], [1, n]])

        act.dma_start(condb[:, :], bcast(cond, B)).then_inc(cond_in, 16)
        act.dma_start(rwraw[:, :, :], router_w.rearrange("(k p) e -> p k e", p=P)).then_inc(router_in, 16)
        act.dma_start(rb[:, 0, :], bcast(router_b, E)).then_inc(router_in, 16)
        act.dma_start(rb[:, 1, :], bcast(router_bias, E)).then_inc(router_in, 16)
        for k, (sb_, eb_) in enumerate(((sb1, eb1), (sb2, eb2))):
            act.dma_start(bstage[0:SH, k, :], sb_.rearrange("(s p) -> s p", p=P)).then_inc(bias_in, 16)
            act.dma_start(bstage[SH:G, k, :], eb_).then_inc(bias_in, 16)
        for half in range(2):
            act.dma_start(sstage[:, 0, half * HN:(half + 1) * HN], log_a_real).then_inc(s4_in, 16)
        act.dma_start(cstage[:, :, :], c_param).then_inc(s4_in, 16)
        act.dma_start(sdt[:, :], bcast(log_dt, C)).then_inc(s4_in, 16)
        for half in range(2):
            act.dma_start(sstage[:, 1, half * HN:(half + 1) * HN], a_imag).then_inc(s4b_in, 16)
        act.dma_start(leni[:, :], bcast(length, B)).then_inc(len_in, 16)
        act.dma_start(ewraw[:, :, :], expert_w.rearrange("(a p) m -> p a m", p=P)).then_inc(l1_in, 16)
        act.dma_start(gwraw[:, :, :], gate_w.rearrange("(k p) e -> p k e", p=P)).then_inc(l1_in, 16)
        wait(act, b3z_ok, 1)
        act.dma_start(b3m[0:1, :], sb3.rearrange("(o n) -> o n", o=1)).then_inc(l1_in, 16)
        act.dma_start(b3m[SH:G, :], eb3).then_inc(l1_in, 16)
        act.dma_start(drow[:, :], d_param.rearrange("(o n) -> o n", o=1)).then_inc(l1_in, 16)
        act.dma_start(fcraw[:, :, :], fc1_w.rearrange("(k p) l -> p k l", p=P)).then_inc(l1_in, 16)
        act.dma_start(fc2raw[:, :, :], fc2_w.rearrange("(a p) n -> p a n", p=P)).then_inc(l1_in, 16)

        wait(act, router_in, 48)
        act.activation(rwh[:, :, :], rwraw[:, :, :], ACT.Copy).then_inc(rw_ok, 1)
        wait(act, s4_in, 64)
        act.activation(sw[:, 1, :], sdt[:, :], ACT.Exp).then_inc(exps_ok, 1)

        for i in range(NT):
            wait(act, mix_done, i + 1)
            act.activation(ah[:, :, i * P:(i + 1) * P], bank[i][:, :].rearrange("p (k n) -> p k n", k=KC), ACT.Copy)\
                .then_inc(ah_ok, 1)

        def split_hi(par, nth, y_needed):
            wait(act, raw_in[par], 48 * nth if isinstance(nth, int) else nth * 48)
            wait(act, y_done, y_needed)
            act.activation(whi[:, par, :], wraw[:, par, :], ACT.Copy).then_inc(whi_ok[par], 1)

        split_hi(0, 1, 0)
        wait(act, tr_done, 2)
        act.activation(spar[:, :, :], bank[2][:, 0:4 * C].rearrange("p (k h) -> p k h", k=4), ACT.Copy)\
            .then_inc(spar_ok, 1)
        wait(act, spar_ok, 1)
        act.activation(sw[:, 0, :], spar[:, 0, :], ACT.Exp).then_inc(exps_ok, 1)
        wait(act, tr_done, 3)
        act.activation(ewt[:, :, :], bank[3][:, 0:LC * LAT].rearrange("p (a l) -> p a l", a=LC), ACT.Copy)\
            .then_inc(ewt_ok, 1)
        wait(act, l1_in, 16 * 7)
        act.activation(gwh[:, :, :], gwraw[:, :, :], ACT.Copy).then_inc(gw_ok, 1)

        def unit(it, r, has_next=True):
            u = it * 4 + r
            par, q = r // 2, r % 2
            if r == 1:
                split_hi(1, it + 1, it * 16)
            if r == 3 and has_next:
                split_hi(0, it + 2, it * 16 + 8)
            if q == 0:
                act.activation(b1cur[:, par:par + 1], b12[:, 0, bass.ds(it * 2 + par, 1)], ACT.Copy)\
                    .then_inc(b1cur_ok, 1)
            wait(act, b1cur_ok, it * 2 + par + 1)
            wait(act, a_done, u + 1)
            wait(act, hid_ok, u - 1)
            act.activation(silu[:, q, :], bank[4 + q][:, :], ACT.Silu, bias=b1cur[:, par:par + 1])\
                .then_inc(silu_ok, 1)
            wait(act, hid_ok, u + 1)
            wait(act, y_done, (u - 1) * 4)
            act.activation(hidh[:, q, :], hid[:, q, :], ACT.Copy).then_inc(hidh_ok, 1)

        wait(act, b12_ok, 1)
        for r in range(2):
            unit(0, r)
        wait(act, soft_in, 1)
        act.activation(w1t[:, :, :], w1t[:, :, :], ACT.Exp).then_inc(soft_out, 1)
        for r in range(2, 4):
            unit(0, r)
        for j in range(2):
            wait(act, gt_done, j + 1)
            act.activation(gt[:, j * HALF:(j + 1) * HALF], bank[4 + j][0:G, :], ACT.Copy).then_inc(gt_ok, 1)

        for n, (lo, hi) in enumerate(FULL_LOOPS):
            with act.Fori(lo, hi) as it:
                for r in range(4):
                    unit(it, r)
            if n == 0:
                wait(act, angle_ok, 1)
                act.activation(angle[:, :, :], angle[:, :, :], ACT.Sin).then_inc(trig_ok, 1)
                act.activation(decay[:, :, :], decay[:, :, :], ACT.Exp, scale=-1.0).then_inc(trig_ok, 1)
            if n == 1:
                for j in range(2):
                    wait(act, k_done, j + 1)
                    act.activation(kout[:, j * 16:(j + 1) * 16, :],
                                   bank[4 + j][0:LI, :].rearrange("p (h j) -> p h j", j=LJ), ACT.Copy)\
                        .then_inc(kout_ok, 1)
        for r in range(4):
            unit(LAST, r, has_next=False)

        wait(act, big_in, 32)
        wait(act, y_done, 16 * ITS)
        for i in range(NT):
            wait(act, y_added, 4 * (4 * ITS - 2) + i + 1 if i < TH else 4 * (4 * ITS - 1) + i % TH + 1)
            wait(act, xt_done, i - 1)
            act.activation(arev[:, i % 2, :], acc[:, i, ::-1], ACT.Copy).then_inc(arev_ok, 1)
        for k in range(KC):
            act.activation(uph[:, k, :], upraw[:, k, :], ACT.Copy).then_inc(uph_ok, 1)
        for g in range(C // 4):
            wait(act, y_ok, g + 1)
            act.activation(ah[:, :, :].rearrange("p k (b h) -> p h k b", h=C)[:, 4 * g:4 * g + 4],
                           ycv[:, g % 2, :, :].rearrange("p h (k b) -> p h k b", k=KC), ACT.Copy).then_inc(yh_ok, 1)
        wait(act, conv_done, C)
        for j in range(JC):
            act.activation(dnh[:, j, :], dnraw[:, j, :], ACT.Copy).then_inc(dnh_ok, 1)
            if j == 0:
                act.activation(fch[:, :, :], fcraw[:, :, :], ACT.Copy).then_inc(fch_ok, 1)
        for a in range(LC):
            wait(act, m2_done, a + 1)
            act.activation(m2h[:, a, :], bank[6 + a][:, :], ACT.Copy).then_inc(m2h_ok, 1)

        for q in range(2):
            for j in range(JC):
                v = q * JC + j
                if v == 0:
                    wait(act, upl_ok, KC)
                wait(act, up_done, v + 1)
                wait(act, sq_ok, v - 1)
                act.activation(rel[:, v % 2, :], bank[4 + v % 2][:, :], ACT.Relu).then_inc(rel_ok, 1)
                wait(act, sq_ok, v + 1)
                wait(act, dn_done, (v - 1) * TH)
                act.activation(sqh[:, v % 2, :], sq[:, v % 2, :], ACT.Copy).then_inc(sqh_ok, 1)
                if j == JC - 1:
                    for a in range(LC):
                        wait(act, lat_done, LC * q + a + 1)
                        wait(act, dnl_ok, JC)
                        wait(act, rt_done, q * TH)
                        act.activation(lath[:, a, :], bank[6 + a][:, :], ACT.Copy).then_inc(lath_ok, 1)
            for i in range(q * TH, (q + 1) * TH):
                wait(act, rt_done, i + 1)
                wait(act, rsc_ok, 1)
                wait(act, osum_ok, i - 1)
                act.activation(routed[:, i % 2, :], bank[4 + i % 4][:, :], ACT.Copy, scale=rsc[:, i:i + 1])\
                    .then_inc(rt_ok, 1)
                wait(act, var_ok, i + 1)
                act.activation(std[:, i:i + 1], mv[:, i, 1:2], ACT.Sqrt, bias=epst[:, :]).then_inc(std_ok, 1)
                wait(act, nmr_ok, i + 1)
                act.activation(osum[:, i % 2, :], osum[:, i % 2, :], ACT.Identity, scale=rstd[:, i:i + 1],
                               bias=nmr[:, i:i + 1]).then_inc(norm_ok, 1)

    @block.vector
    def _(dve):
        steps = [0]

        def link(ins):
            steps[0] += 1
            ins.then_inc(vec_step, 1)
            dve.wait_ge(vec_step, steps[0])

        tt = dve.tensor_tensor
        dve.memset(gates[:, 0:SH, :], 1.0).then_inc(gates_ok, 1)
        dve.memset(b3m[:, :], 0.0).then_inc(b3z_ok, 1)
        link(dve.memset(wbd[:, :, :], 0.0))
        dve.wait_ge(cpart_ok, 1)
        link(dve.tensor_scalar(cpart[:, :], cpart[:, :], C - 1, None, ALU.bitwise_and))
        dve.wait_ge(cond_in, 16)
        for b in range(BT):
            s = slice(b * C, (b + 1) * C)
            link(dve.tensor_scalar(cidx[s, :], condb[s, b::BT], C, None, ALU.mult))
        tt(cidx[:, :], cidx[:, :], cpart[:, :], ALU.add).then_inc(cidx_ok, 1)
        dve.wait_ge(wsel_in, 16 * NT)
        for b in range(BT):
            s = slice(b * C, (b + 1) * C)
            dve.tensor_copy(wbd[s, :, s], wsel[s, :, :]).then_inc(wbd_ok, 1)
        dve.wait_ge(rw_ok, 1)
        tt(rwl[:, :, :], rwraw[:, :, :], f(rwh[:, :, :]), ALU.subtract).then_inc(rw_ok, 1)
        for i in range(NT):
            dve.wait_ge(ah_ok, i + 1)
            tt(al[:, :, i * P:(i + 1) * P], bank[i][:, :].rearrange("p (k n) -> p k n", k=KC),
               f(ah[:, :, i * P:(i + 1) * P]), ALU.subtract).then_inc(al_ok, 1)

        def split_lo(par, nth, y_needed):
            wait(dve, whi_ok[par], nth)
            wait(dve, y_done, y_needed)
            tt(wlo[:, par, :], wraw[:, par, :], f(whi[:, par, :]), ALU.subtract).then_inc(wlo_ok[par], 1)

        split_lo(0, 1, 0)
        dve.wait_ge(tr_done, 1)
        dve.tensor_copy(b12[:, :, :], bank[1][:, 0:2 * G].rearrange("p (k g) -> p k g", k=2)).then_inc(b12_ok, 1)

        def tiles(ap, n):
            return ap.unsqueeze(2).broadcast_to([P, NT, n])

        def rows(ap, n):
            return ap.unsqueeze(1).broadcast_to([P, NT, n])

        dve.wait_ge(lg_done, 1)
        link(tt(sc[:, :, :], bank[0][:, 0:NT * E].rearrange("p (i e) -> p i e", e=E), rows(rb[:, 0, :], E), ALU.add))

        def add_y(uy, it_y, r_y, i):
            par, q = r_y // 2, r_y % 2
            tile = q * TH + i
            wait(dve, y_done, uy * 4 + i + 1)
            wait(dve, y_added, uy * 4 + i - 7)
            gate = gates[:, :, :].rearrange("p g i -> p (g i)")[:, bass.ds((it_y * 2 + par) * NT + tile, 1)]
            dve.scalar_tensor_tensor(acc[:, tile, :], bank[i][:, :], gate, acc[:, tile, :], ALU.mult, ALU.add)\
                .then_inc(y_added, 1)

        def unit(it, r, has_next=True):
            u = it * 4 + r
            par, q = r // 2, r % 2
            before = (it, r - 1) if r else (it - 1, 3)
            first = isinstance(u, int) and u == 0
            if r == 1:
                split_lo(1, it + 1, it * 16)
            if r == 3 and has_next:
                split_lo(0, it + 2, it * 16 + 8)
            wait(dve, c_done, u + 1)
            wait(dve, silu_ok, u + 1)
            wait(dve, hidh_ok, u - 1)
            wait(dve, hidl_ok, u - 1)
            dve.scalar_tensor_tensor(hid[:, q, :], bank[6 + q][:, :], b12[:, 1, bass.ds(it * 2 + par, 1)],
                                     silu[:, q, :], ALU.add, ALU.mult).then_inc(hid_ok, 1)
            if not first:
                add_y(u - 1, *before, 0)
            wait(dve, hidh_ok, u + 1)
            wait(dve, y_done, (u - 1) * 4)
            tt(hidl[:, q, :], hid[:, q, :], f(hidh[:, q, :]), ALU.subtract).then_inc(hidl_ok, 1)
            if not first:
                for i in range(1, TH):
                    add_y(u - 1, *before, i)

        dve.wait_ge(b12_ok, 1)
        for r in range(2):
            unit(0, r)

        def first_max(dst, src, tmp, n):
            link(dve.tensor_reduce(red[:, 0, :], src, AX.X, ALU.max))
            link(tt(tmp, src, tiles(red[:, 0, :], n), ALU.is_equal))
            link(tt(tmp, tmp, rows(desc[:, 0:n], n), ALU.mult))
            link(dve.tensor_reduce(red[:, 1, :], tmp, AX.X, ALU.max))
            link(tt(dst, tmp, tiles(red[:, 1, :], n), ALU.is_equal))

        link(dve.tensor_reduce(red[:, 0, :], sc[:, :, :], AX.X, ALU.max))
        tt(w1t[:, :, :], sc[:, :, :], tiles(red[:, 0, :], E), ALU.subtract).then_inc(soft_in, 1)
        dve.wait_ge(soft_out, 1)
        link(dve.tensor_reduce(red[:, 0, :], w1t[:, :, :], AX.X, ALU.add))
        link(dve.reciprocal(red[:, 1, :], red[:, 0, :]))
        link(tt(sc[:, :, :], w1t[:, :, :], tiles(red[:, 1, :], E), ALU.mult))
        link(tt(sc[:, :, :], sc[:, :, :], rows(rb[:, 1, :], E), ALU.add))
        link(dve.tensor_reduce(gm[:, :, :], sc[:, :, :].rearrange("p i (g e) -> p i g e", g=NG), AX.X, ALU.max))
        dve.wait_ge(desc_ok, 1)
        first_max(oh1[:, :, 0:NG], gm[:, :, :], w1t[:, :, 0:NG], NG)
        link(dve.scalar_tensor_tensor(gm[:, :, :], oh1[:, :, 0:NG], -BIG, gm[:, :, :], ALU.mult, ALU.add))
        first_max(oh2[:, :, 0:NG], gm[:, :, :], w1t[:, :, 0:NG], NG)
        link(tt(keep[:, :, :], oh1[:, :, 0:NG], oh2[:, :, 0:NG], ALU.add))
        link(dve.tensor_scalar(keep[:, :, :], keep[:, :, :], -1.0, BIG, ALU.add, ALU.mult))
        link(tt(w2t[:, :, :].rearrange("p i (g e) -> p i g e", g=NG), sc[:, :, :].rearrange("p i (g e) -> p i g e", g=NG),
                keep[:, :, :].unsqueeze(3).broadcast_to([P, NT, NG, E // NG]), ALU.add))
        first_max(oh1[:, :, :], w2t[:, :, :], w1t[:, :, :], E)
        link(dve.scalar_tensor_tensor(w2t[:, :, :], oh1[:, :, :], -BIG, w2t[:, :, :], ALU.mult, ALU.add))
        first_max(oh2[:, :, :], w2t[:, :, :], w1t[:, :, :], E)
        link(tt(oh1[:, :, :], oh1[:, :, :], oh2[:, :, :], ALU.add))
        tt(gates[:, SH:G, :].rearrange("p e i -> p i e"), oh1[:, :, :], sc[:, :, :], ALU.mult).then_inc(gates_ok, 1)

        for r in range(2, 4):
            unit(0, r)
        for i in range(NT):
            wait(dve, b3_done, i + 1)
            wait(dve, y_added, 12)
            tt(acc[:, i, :], bank[i % 4][:, :], acc[:, i, :], ALU.add).then_inc(b3_added, 1)
        dve.wait_ge(dim_ok, 1)
        dve.tensor_copy(dimh[:, :], sw[:, 3, :]).then_inc(dimh_ok, 1)
        dve.reciprocal(sw[:, 6, :], sw[:, 5, :]).then_inc(rden_ok, 1)
        dve.wait_ge(lenf_ok, 1)
        tt(mask[:, :, :, :].rearrange("p r k b -> p (r k) b"), lenf[:, :].unsqueeze(1).broadcast_to([P, 2 * KC, B]),
           tpos[:, :, :].rearrange("p r k -> p (r k)").unsqueeze(2).broadcast_to([P, 2 * KC, B]), ALU.is_gt)\
            .then_inc(mask_ok, 1)
        dve.wait_ge(gw_ok, 1)
        tt(gwl[:, :, :], gwraw[:, :, :], f(gwh[:, :, :]), ALU.subtract).then_inc(gw_ok, 1)
        wait(dve, b3_added, NT)

        for lo, hi in FULL_LOOPS:
            with dve.Fori(lo, hi) as it:
                for r in range(4):
                    unit(it, r)
        for r in range(4):
            unit(LAST, r, has_next=False)
        for i in range(TH):
            add_y(4 * ITS - 1, LAST, 3, i)

        dve.wait_ge(mask_ok, 1)
        for i in range(NT):
            wait(dve, xt_done, i + 1)
            tt(u_t[:, :, :, BT * i:BT * i + BT].rearrange("p h k b -> p k b h"),
               bank[4 + i % 4][:, :].rearrange("p (k b h) -> p k b h", k=KC, b=BT),
               mask[:, 1, :, BT * i:BT * i + BT].unsqueeze(3).broadcast_to([P, KC, BT, C]), ALU.mult).then_inc(u_ok, 1)

        def y_lo(g):
            wait(dve, yh_ok, g + 1)
            tt(al[:, :, :].rearrange("p k (b h) -> p h k b", h=C)[:, 4 * g:4 * g + 4],
               ycv[:, g % 2, :, :].rearrange("p h (k b) -> p h k b", k=KC),
               f(ah[:, :, :]).rearrange("p k (b h) -> p h k b", h=C)[:, 4 * g:4 * g + 4], ALU.subtract)\
                .then_inc(yl_ok, 1)

        for g in range(C // 4):
            wait(dve, conv_done, 4 * g + 4)
            wait(dve, yh_ok, g - 1)
            wait(dve, yl_ok, g - 1)
            tt(ycv[:, g % 2, :, :], bank[g % 4][:, :].rearrange("p (h n) -> p h n", h=4),
               mask[:, 0, :, :].rearrange("p k b -> p (k b)").unsqueeze(1).broadcast_to([P, 4, P]), ALU.mult)\
                .then_inc(y_ok, 1)
            if g:
                y_lo(g - 1)
        y_lo(C // 4 - 1)
        for a in range(LC):
            wait(dve, m2h_ok, a + 1)
            tt(m2l[:, a, :], bank[6 + a][:, :], f(m2h[:, a, :]), ALU.subtract).then_inc(m2l_ok, 1)
        wait(dve, lg1_done, 1)
        for i in range(NT):
            dve.max(top8[:, i, :], bank[5][:, i * NE1:(i + 1) * NE1]).then_inc(top_ok, 1)
        wait(dve, top_ok, NT)
        tt(rsc[:, :], top8[:, :, 0], top8[:, :, 1], ALU.add).then_inc(rsc_ok, 1)

        for q in range(2):
            for j in range(JC):
                v = q * JC + j
                wait(dve, rel_ok, v + 1)
                wait(dve, sqh_ok, v - 1)
                wait(dve, sql_ok, v - 1)
                tt(sq[:, v % 2, :], rel[:, v % 2, :], rel[:, v % 2, :], ALU.mult).then_inc(sq_ok, 1)
                wait(dve, sqh_ok, v + 1)
                wait(dve, dn_done, (v - 1) * TH)
                tt(sql[:, v % 2, :], sq[:, v % 2, :], f(sqh[:, v % 2, :]), ALU.subtract).then_inc(sql_ok, 1)
                if j == JC - 1:
                    for a in range(LC):
                        wait(dve, lath_ok, LC * q + a + 1)
                        tt(latl[:, a, :], bank[6 + a][:, :], f(lath[:, a, :]), ALU.subtract).then_inc(latl_ok, 1)
            for i in range(q * TH, (q + 1) * TH):
                o = osum[:, i % 2, :]
                wait(dve, rt_ok, i + 1)
                wait(dve, dn_done, 4 * (JC * (q + 1) - 1) + i % TH + 1)
                wait(dve, fin_ok, i - 1)
                tt(o, bank[i % TH][:, :], routed[:, i % 2, :], ALU.add).then_inc(osum_ok, 1)
                wait(dve, osum_ok, i + 1)
                link(dve.bn_stats(stats[:, i, :], o))
                dve.bn_aggr(mv[:, i, :], stats[:, i, :]).then_inc(var_ok, 1)
                wait(dve, std_ok, i + 1)
                link(dve.reciprocal(rstd[:, i:i + 1], std[:, i:i + 1]))
                dve.scalar_tensor_tensor(nmr[:, i:i + 1], mv[:, i, 0:1], -1.0, rstd[:, i:i + 1], ALU.mult, ALU.mult)\
                    .then_inc(nmr_ok, 1)
                wait(dve, norm_ok, i + 1)
                if i == 0:
                    wait(dve, ln_in, 32)
                link(tt(o, o, gam[:, :], ALU.mult))
                wait(dve, resid_ok, i + 1)
                tt(acc[:, i, :], o, acc[:, i, :], ALU.add).then_inc(fin_ok, 1)

    @block.tensor
    def _(pe):
        wait(pe, wbd_ok, BT)
        for i in range(NT):
            wait(pe, x_in[i // 2], 16)
            for k in range(KC):
                mm = pe.matmul(bank[i][:, k * P:(k + 1) * P], acc[:, i, k * P:(k + 1) * P], wbd[:, i, :],
                               start=True, stop=True)
            mm.then_inc(mix_done, 1)
        wait(pe, ident_ok, 1)
        wait(pe, rw_ok, 2)
        for i in range(NT):
            wait(pe, ah_ok, i + 1)
            wait(pe, al_ok, i + 1)
            s = slice(i * P, (i + 1) * P)
            mm = split3(pe, bank[0][:, i * E:(i + 1) * E], lambda k: (ah[:, k, s], al[:, k, s]),
                        lambda k: (rwh[:, k, :], rwl[:, k, :]), KC)
        mm.then_inc(lg_done, 1)
        wait(pe, bias_in, 64)
        for k in range(2):
            mm = pe.matmul(bank[1][:, k * G:(k + 1) * G], bstage[:, k, :], ident[0:G, 0:G], start=True, stop=True)
        mm.then_inc(tr_done, 1)
        wait(pe, s4b_in, 32)
        wait(pe, s4_in, 64)
        wait(pe, stage_ok, 1)
        for k in range(4):
            mm = pe.matmul(bank[2][:, k * C:(k + 1) * C], sstage[:, k, :], ident[0:C, 0:C], start=True, stop=True)
        mm.then_inc(tr_done, 1)
        wait(pe, l1_in, 16 * 7)
        for m in range(LC):
            for l in range(LC):
                mm = pe.matmul(bank[3][:, m * LAT + l * P:m * LAT + (l + 1) * P], ewraw[:, l, m * P:(m + 1) * P],
                               ident[:, :], start=True, stop=True)
        mm.then_inc(tr_done, 1)

        def y_products(uy, r_y):
            par, q = r_y // 2, r_y % 2
            wait(pe, hidh_ok, uy + 1)
            wait(pe, hidl_ok, uy + 1)
            w3 = slice(2 * KC * P, WCOLS)
            for i in range(TH):
                s = slice(i * P, (i + 1) * P)
                wait(pe, y_added, uy * 4 + i - 3)
                split3(pe, bank[i][:, :], lambda k: (hidh[:, q, s], hidl[:, q, s]),
                       lambda k: (whi[:, par, w3], wlo[:, par, w3]), 1).then_inc(y_done, 1)

        def unit(it, r):
            u = it * 4 + r
            par, q = r // 2, r % 2
            wait(pe, whi_ok[par], it + 1)
            wait(pe, wlo_ok[par], it + 1)
            tok = slice(q * HALF, (q + 1) * HALF)
            for off, ready, sem_done, dst in ((0, silu_ok, a_done, 4), (KC, hid_ok, c_done, 6)):
                wait(pe, ready, u - 1)
                split3(pe, bank[dst + q][:, :],
                       lambda k: (whi[:, par, (off + k) * P:(off + k + 1) * P],
                                  wlo[:, par, (off + k) * P:(off + k + 1) * P]),
                       lambda k: (ah[:, k, tok], al[:, k, tok]), KC).then_inc(sem_done, 1)
            if not (isinstance(u, int) and u == 0):
                y_products(u - 1, (r - 1) % 4)

        wait(pe, b12_ok, 1)
        wait(pe, spar_ok, 1)
        wait(pe, ewt_ok, 1)
        for r in range(4):
            unit(0, r)
        wait(pe, gates_ok, 2)
        for j in range(2):
            wait(pe, silu_ok, 3 + j)
            for i in range(TH):
                mm = pe.matmul(bank[4 + j][0:G, i * P:(i + 1) * P], gates[:, :, j * TH + i], ident[:, :],
                               start=True, stop=True)
            mm.then_inc(gt_done, 1)
        wait(pe, gt_ok, 2)
        wait(pe, y_added, 12)
        for i in range(NT):
            wait(pe, b3_added, i - 3)
            pe.matmul(bank[i % 4][:, :], gt[:, i * P:(i + 1) * P], b3m[:, :], start=True, stop=True).then_inc(b3_done, 1)
        wait(pe, b3_added, NT)

        for n, (lo, hi) in enumerate(FULL_LOOPS):
            with pe.Fori(lo, hi) as it:
                for r in range(4):
                    unit(it, r)
            if n == 1:
                wait(pe, lhs_ok, 1)
                for j in range(2):
                    wait(pe, silu_ok, 4 * hi - 1 + j)
                    for h in range(16 * j, 16 * j + 16):
                        c = (h % 16) * LJ
                        mm = pe.matmul(bank[4 + j][0:LI, c:c + LJ], lhs_k[:, h, :], term[:, h, 2 * LI:2 * LI + LJ],
                                       start=True, stop=True)
                    mm.then_inc(k_done, 1)
                wait(pe, kout_ok, 2)
        for r in range(4):
            unit(LAST, r)
        y_products(4 * ITS - 1, 3)

        for i in range(NT):
            wait(pe, silu_ok, 4 * ITS)
            wait(pe, hid_ok, 4 * ITS)
            wait(pe, arev_ok, i + 1)
            wait(pe, u_ok, i - 3)
            for k in range(KC):
                mm = pe.matmul(bank[4 + i % 4][:, k * P:(k + 1) * P], arev[:, i % 2, (KC - 1 - k) * P:(KC - k) * P], ident[:, :],
                               start=True, stop=True)
            mm.then_inc(xt_done, 1)
        wait(pe, u_ok, NT)
        for h in range(C):
            if h == 0:
                wait(pe, toep_in[0], 32)
            if h == TS:
                wait(pe, toep_in[1], 16)
            if h % 4 == 0:
                wait(pe, y_ok, h // 4 - 3)
            for d in range(KC):
                c = (h % 4) * P
                mm = pe.matmul(bank[h // 4 % 4][:, c + d * B:c + P], toep[:, h % TS, d * P:(d + 1) * P],
                               u_t[:, h, 0:KC - d, :].rearrange("p k b -> p (k b)"), start=(d == 0), stop=(d == KC - 1))
            mm.then_inc(conv_done, 1)
        for a in range(LC):
            for m in range(LC):
                mm = pe.matmul(bank[6 + a][:, :], ewt[:, m, a * P:(a + 1) * P], fc2raw[:, m, :],
                               start=(m == 0), stop=(m == LC - 1))
            mm.then_inc(m2_done, 1)
        wait(pe, yh_ok, C // 4)
        wait(pe, yl_ok, C // 4)
        wait(pe, gw_ok, 2)
        for i in range(NT):
            s = slice(i * P, (i + 1) * P)
            mm = split3(pe, bank[5][:, i * NE1:(i + 1) * NE1], lambda k: (ah[:, k, s], al[:, k, s]),
                        lambda k: (gwh[:, k, :], gwl[:, k, :]), KC)
        mm.then_inc(lg1_done, 1)

        def down(v):
            q, j = v // JC, v % JC
            wait(pe, sqh_ok, v + 1)
            wait(pe, sql_ok, v + 1)
            wait(pe, dnh_ok, j + 1)
            wait(pe, dnl_ok, j + 1)
            for i in range(TH):
                s = slice(i * P, (i + 1) * P)
                if j == 0:
                    wait(pe, osum_ok, (q - 1) * TH + i + 1)
                pe.matmul(bank[i][:, :], sqh[:, v % 2, s], dnh[:, j, :], start=(j == 0), stop=False)
                pe.matmul(bank[i][:, :], sqh[:, v % 2, s], dnl[:, j, :], start=False, stop=False)
                pe.matmul(bank[i][:, :], sql[:, v % 2, s], dnh[:, j, :], start=False, stop=(j == JC - 1))\
                    .then_inc(dn_done, 1)

        wait(pe, uph_ok, KC)
        wait(pe, upl_ok, KC)
        for q in range(2):
            tok = slice(q * HALF, (q + 1) * HALF)
            for j in range(JC):
                v = q * JC + j
                s = slice(j * P, (j + 1) * P)
                if v == 1:
                    wait(pe, top_ok, NT)
                if j < 2:
                    wait(pe, rt_ok, q * TH)
                wait(pe, rel_ok, v - 1)
                split3(pe, bank[4 + v % 2][:, :], lambda k: (uph[:, k, s], upl[:, k, s]),
                       lambda k: (ah[:, k, tok], al[:, k, tok]), KC).then_inc(up_done, 1)
                if j:
                    down(v - 1)
            wait(pe, fch_ok, 1)
            wait(pe, fcl_ok, 1)
            wait(pe, m2l_ok, LC)
            for a in range(LC):
                s = slice(a * P, (a + 1) * P)
                split3(pe, bank[6 + a][:, :], lambda k: (fch[:, k, s], fcl[:, k, s]),
                       lambda k: (ah[:, k, tok], al[:, k, tok]), KC).then_inc(lat_done, 1)
            down(q * JC + JC - 1)
            wait(pe, lath_ok, LC * (q + 1))
            wait(pe, latl_ok, LC * (q + 1))
            wait(pe, rel_ok, (q + 1) * JC)
            for i in range(TH):
                s = slice(i * P, (i + 1) * P)
                split3(pe, bank[4 + i][:, :], lambda a: (lath[:, a, s], latl[:, a, s]),
                       lambda a: (m2h[:, a, :], m2l[:, a, :]), LC).then_inc(rt_done, 1)

    ctx.close()


_INS = ["x", "itok_B_0_15", "itok_B_8_3872", "L0_cond_weights", "L0_ffn_router_w", "L0_ffn_router_b",
        "L0_ffn_router_bias", "L0_ffn_ew1", "L0_ffn_eb1", "L0_ffn_ew2", "L0_ffn_eb2", "L0_ffn_ew3", "L0_ffn_eb3",
        "L0_ffn_sw1", "L0_ffn_sb1", "L0_ffn_sw2", "L0_ffn_sb2", "L0_ffn_sw3", "L0_ffn_sb3", "L1_cond_log_dt",
        "L1_cond_C", "L1_cond_log_A_real", "L1_cond_A_imag", "L1_cond_D", "L1_ffn_gate_w", "L1_ffn_up_w",
        "L1_ffn_down_w", "L1_ffn_fc1_w", "L1_ffn_fc2_w", "L1_ffn_expert_w", "L1_ffn_ln_gamma", "L1_ffn_ln_beta"]


def kernel(**inputs):
    import concourse.bacc as bacc
    from concourse.bass_utils import run_bass_kernel_spmd

    nc = bacc.Bacc("TRN2", target_bir_lowering=False, num_devices=1)
    arrays, args = {}, []
    for name in _INS:
        a = np.ascontiguousarray(inputs[name])
        arrays[f"in_{name}"] = a
        args.append(nc.dram_tensor(f"in_{name}", a.shape, mybir.dt.from_np(a.dtype), kind="ExternalInput").ap())
    res = nc.dram_tensor("out_0", inputs["x"].shape, F32, kind="ExternalOutput").ap()
    adaln_ffn_program(nc, *args, res)
    r = run_bass_kernel_spmd(nc, [arrays], core_ids=[0])
    return r.results[0]["out_0"]
```

```python
import math
from contextlib import ExitStack

import concourse.bass as bass
import numpy as np
from concourse import mybir

F32 = mybir.dt.float32
F32R = mybir.dt.float32r
I32 = mybir.dt.int32
U32 = mybir.dt.uint32
ALU = mybir.AluOpType
ACT = mybir.ActivationFunctionType
AX = mybir.AxisListType

P = 128
MAGIC = 1.5 * 2.0 ** 23
BIG = 3.0e38
LN_EPS = 1e-5
PI_1 = 6.28125
PI_2 = float(np.float32(2 * math.pi - PI_1))
PI_SAFE = 3.1415925
FLOOR = 127 / 256


def adaln_ffn_program(nc, x, cond, length, cond_w, router_w, router_b, router_bias, ew1, eb1, ew2, eb2, ew3, eb3,
                      sw1, sb1, sw2, sb2, sw3, sb3, log_dt, c_param, log_a_real, a_imag, d_param,
                      gate_w, up_w, down_w, fc1_w, fc2_w, expert_w, ln_gamma, ln_beta, out):
    B, C, T = x.shape
    N = B * C
    NT = N // P
    KC = T // P
    BT = P // C
    HALF = N // 2
    TH = NT // 2
    E, _, INTER = ew1.shape
    SH = sw1.shape[1] // INTER
    G = SH + E
    K = 2
    NB = (K * N - E) // P + E
    NSLOT = 32
    NG = 4
    INT1 = up_w.shape[1]
    JC = INT1 // P
    LAT = fc1_w.shape[1]
    LC = LAT // P
    NE1 = gate_w.shape[1]
    HN = a_imag.shape[1]
    LI = 16
    LJ = T // LI
    NL = 2 * LI + LJ + 2
    PAD = P + T
    TS = 24
    WCOLS = 2 * KC * INTER + T
    M2_AFTER = (1, 3, 5, 6)
    XT_BANK = (4, 5, 4, 5, 2, 3, 4, 5)
    YS = 8
    WARM = 7
    RAWS = 4
    assert NB == 8 * RAWS - 1
    assert NB == NSLOT - 1 and INTER == P and SH == 2 and 2 * HN == P and G % 2 == 0

    xrow = nc.dram_tensor("xrow", [N, T], F32).ap()
    ysort = nc.dram_tensor("ysort", [NB * P, T], F32).ap()
    bsplit = nc.dram_tensor("bsplit", [E, 2, 2 * P], F32R).ap()
    kpad = nc.dram_tensor("kpad", [C, PAD], F32).ap()

    base = 16512
    cursor = [base]

    def region(size):
        at = cursor[0]
        cursor[0] += size
        return [at]

    def at(reg, name, shape, dt=F32):
        width = int(np.prod(shape[1:])) * 4
        t = nc.alloc_sbuf_tensor_at(name, shape, dt, offset=reg[0])
        reg[0] += (width + 31) // 32 * 32
        return t

    main = region(3 * NT * T * 4)
    acc = at(main, "acc", [P, NT, T])
    ah = at(main, "ah", [P, KC, N], F32R)
    al = at(main, "al", [P, KC, N], F32R)
    toep_at = cursor[0]
    toep_reg = region(TS * T * 4)
    toep = at(toep_reg, "toep", [P, TS, T])
    exp_at = cursor[0]
    exp_reg = region((6 * WCOLS + 8 * HALF) * 4)
    wraw = at(exp_reg, "wraw", [P, 2, WCOLS])
    whi = at(exp_reg, "whi", [P, 2, WCOLS], F32R)
    wlo = at(exp_reg, "wlo", [P, 2, WCOLS], F32R)
    r = list(exp_reg)
    xstage = at(r, "xstage", [P, 4, T])
    silu = at(exp_reg, "silu", [P, 2, HALF])
    r = [exp_at + 2 * WCOLS * 4]
    warm = at(r, "warm", [P, T])
    hid = at(exp_reg, "hid", [P, 2, HALF])
    hidh = at(exp_reg, "hidh", [P, 2, HALF], F32R)
    hidl = at(exp_reg, "hidl", [P, 2, HALF], F32R)
    raw_at = cursor[0]
    raw_reg = region(2 * KC * INT1 * 4)
    upraw = at(raw_reg, "upraw", [P, KC, INT1])
    dnraw = at(raw_reg, "dnraw", [P, JC, T])
    r = [toep_at]
    decay = at(r, "decay", [P, C, NL])
    turns = at(r, "turns", [P, C, NL])
    term = at(r, "term", [P, C, NL])
    angle = at(r, "angle", [P, C, NL])
    lhs_k = at(r, "lhs_k", [P, C, LI])
    tmp_k = at(r, "tmp_k", [P, C, LI])
    kout = at(r, "kout", [LI, C, LJ])
    tri = at(r, "tri", [P, P])
    ones = at(r, "ones", [P, P])
    cmp = at(r, "cmp", [1, NSLOT, E])
    browb = at(r, "browb", [1, 2, 2, 2 * P], F32R)
    assert r[0] <= toep_reg[0]
    r = [toep_at + (C - TS) * T * 4]
    dnh = at(r, "dnh", [P, JC, T], F32R)
    dnl = at(r, "dnl", [P, JC, T], F32R)
    assert r[0] <= toep_reg[0]
    r = [toep_at]
    ltg = at(r, "ltg", [2 * NE1, 2, HALF])
    latf = at(r, "latf", [P, LC, HALF])
    rscb = at(r, "rscb", [P, 2, HALF])
    assert r[0] <= toep_at + (C - TS) * T * 4
    r = [exp_at + 2 * KC * INT1 * 4]
    m2h = at(r, "m2h", [P, LC, T], F32R)
    m2l = at(r, "m2l", [P, LC, T], F32R)
    fch = at(r, "fch", [P, KC, LAT], F32R)
    fcl = at(r, "fcl", [P, KC, LAT], F32R)
    r = [exp_at]
    uph = at(r, "uph", [P, KC, INT1], F32R)
    upl = at(r, "upl", [P, KC, INT1], F32R)
    u_t = at(r, "u_t", [P, C, KC, B])
    r = [raw_at]
    wbd = at(r, "wbd", [P, NT, P])
    wsel = at(r, "wsel", [P, NT, C])
    bstage = at(r, "bstage", [G, 2, P])
    sstage = at(r, "sstage", [C, 4, P])
    cstage = at(r, "cstage", [C, HN, 2])
    bexp = at(r, "bexp", [E, 2 * P])
    bexh = at(r, "bexh", [E, 2 * P], F32R)
    bexl = at(r, "bexl", [E, 2 * P], F32R)
    assert r[0] <= raw_at + 2 * WCOLS * 4
    r = [raw_at]
    wrawx = at(r, "wrawx", [P, 2, WCOLS])
    ewraw = at(r, "ewraw", [P, LC, LAT])
    before = at(r, "before", [P, E, E])
    blk = at(r, "blk", [P, 3, E])
    zrow = at(r, "zrow", [C, P])
    assert r[0] <= raw_at + KC * INT1 * 4
    r = [raw_at]
    sc = at(r, "sc", [P, NT, E])
    r2 = list(r)
    w1t = at(r, "w1t", [P, NT, E])
    w2t = at(r, "w2t", [P, NT, E])
    w12t = at(r2, "w12t", [P, K, NT, E])
    oh = at(r, "oh", [P, K, NT, E])
    rank = at(r, "rank", [P, NT, E])
    pre = at(r, "pre", [P, NT + 1, E])
    nbef = at(r, "nbef", [P, E, E])
    assert r[0] <= raw_at + (NT * P + NT * C) * 4
    r = [raw_at + KC * INT1 * 4]
    ltr = at(r, "ltr", [2 * E, 2, HALF])
    r = [raw_at + KC * INT1 * 4]
    hotp = at(r, "hotp", [P, K * NT, P], F32R)
    hotb = at(r, "hotb", [P, K * NT, NSLOT], F32R)
    hott = at(r, "hott", [P, K * NT, NSLOT])
    r = [raw_at + KC * INT1 * 4]
    xg = at(r, "xg", [P, RAWS, T])
    r = [exp_at + 6 * WCOLS * 4]
    xth = at(r, "xth", [P, 2, KC, P], F32R)
    xtl = at(r, "xtl", [P, 2, KC, P], F32R)
    bsil = at(r, "bsil", [P, 2, P])
    bhid = at(r, "bhid", [P, 2, P])
    bhh = at(r, "bhh", [P, 2, P], F32R)
    bhl = at(r, "bhl", [P, 2, P], F32R)
    yout = at(r, "yout", [P, 2, T])
    assert r[0] <= exp_reg[0]
    r = [raw_at + KC * INT1 * 4]
    yg = at(r, "yg", [P, YS, T])
    r = [raw_at]
    rel = at(r, "rel", [P, 2, HALF])
    sqh = at(r, "sqh", [P, 2, HALF], F32R)
    sql = at(r, "sql", [P, 2, HALF], F32R)
    r = [raw_at + KC * INT1 * 4]
    lath = at(r, "lath", [P, LC, HALF], F32R)
    latl = at(r, "latl", [P, LC, HALF], F32R)
    osum = at(r, "osum", [P, TH, T])
    r = [exp_at + 2 * KC * INT1 * 4 + N * KC * 4]
    ycv = at(r, "ycv", [P, 2, 4, P])
    r = [exp_at]
    arev = at(r, "arev", [P, 2, T])
    r = [exp_at + 2 * KC * INT1 * 4 + N * KC * 4]
    sq = at(r, "sq", [P, 2, HALF])

    small = [cursor[0]]
    ident = at(small, "ident", [P, P])
    onesr = at(small, "onesr", [1, P], F32R)
    prow = at(small, "prow", [P, P])
    r = list(small)
    browa = at(r, "browa", [1, 2, 2, 2 * P], F32R)
    r = list(small)
    gt = at(small, "gt", [G, N])
    gam = at(r, "gam", [P, T])
    bet = at(r, "bet", [P, T])
    b3m = at(small, "b3m", [G, T])
    fcraw = at(small, "fcraw", [P, KC, LAT])
    fc2raw = at(small, "fc2raw", [P, LC, T])
    ewt = at(small, "ewt", [P, LC, LAT])
    rwraw = at(small, "rwraw", [P, KC, E])
    rwc = at(small, "rwc", [P, KC, 2 * E], F32R)
    gwraw = at(small, "gwraw", [P, KC, NE1])
    gwc = at(small, "gwc", [P, KC, 2 * NE1], F32R)
    lg1 = at(small, "lg1", [P, NT, NE1])
    rb = at(small, "rb", [P, 2, E])
    b12 = at(small, "b12", [P, 2, G])
    gates = at(small, "gates", [P, G, NT])
    gm = at(small, "gm", [P, NT, NG])
    keep = at(small, "keep", [P, NT, NG])
    desc = at(small, "desc", [P, E])
    desci = at(small, "desci", [P, E], I32)
    tokf = at(small, "tokf", [P, NT])
    ejf = at(small, "ejf", [1, NSLOT])
    eji = at(small, "eji", [1, NSLOT], I32)
    slot = at(small, "slot", [P, K, NT])
    sblk = at(small, "sblk", [P, K, NT])
    srem = at(small, "srem", [P, K, NT])
    gk = at(small, "gk", [P, K, NT])
    sloti = at(small, "sloti", [P, K, NT], I32)
    tokx = at(small, "tokx", [P, NSLOT], I32)
    cidx = at(small, "cidx", [P, NT], I32)
    condb = at(small, "condb", [P, B], I32)
    cpart = at(small, "cpart", [P, NT], I32)
    red = at(small, "red", [P, 2, NT])
    leni = at(small, "leni", [P, B], I32)
    lenf = at(small, "lenf", [P, B])
    tpos = at(small, "tpos", [P, 2, KC])
    tposi = at(small, "tposi", [P, 2, KC], I32)
    mask = at(small, "mask", [P, 2, KC, B])
    spar = at(small, "spar", [P, 4, C])
    sdt = at(small, "sdt", [P, C])
    sw = at(small, "sw", [P, 14, C])
    dimh = at(small, "dimh", [P, C], F32R)
    lvals = at(small, "lvals", [P, NL])
    lvali = at(small, "lvali", [P, NL], I32)
    lturn = at(small, "lturn", [P, NL])
    shq = at(small, "shq", [P, NL])
    shr = at(small, "shr", [P, NL])
    drow = at(small, "drow", [1, C])
    top8 = at(small, "top8", [P, NT, 8])
    rsc = at(small, "rsc", [P, NT])
    stats = at(small, "stats", [P, NT, 6])
    mv = at(small, "mv", [P, NT, 2])
    std = at(small, "std", [P, NT])
    rstd = at(small, "rstd", [P, NT])
    nmr = at(small, "nmr", [P, NT])
    epst = at(small, "epst", [P, 1])
    assert small[0] <= nc.sbuf_usable_end, (small, nc.sbuf_usable_end)

    bank = [nc.alloc_psum_tensor(f"bank{i}", [P, 512], F32) for i in range(8)]

    ctx = ExitStack()

    def sem(name):
        return ctx.enter_context(nc.semaphore(name))

    xrow_out, bsplit_out = [sem("xrow_out0"), sem("xrow_out1")], sem("bsplit_out")
    xg_in = [sem(f"xg_in{k}") for k in range(RAWS)]
    ys_out = [sem(f"ys_out{k}") for k in range(2)]
    raw_in = [sem(f"raw_in{k}") for k in range(RAWS)]
    sraw_in, swh_ok, swl_ok = sem("sraw_in"), sem("swh_ok"), sem("swl_ok")
    yg_in = [sem(f"yg_in{k}") for k in range(YS)]
    bexp_in = sem("bexp_in")
    x_in = [sem(f"x_in{i}") for i in range(4)]
    wsel_in = [sem("wsel_in0"), sem("wsel_in1")]
    cond_in, bias_in, router_in, s4_in, s4b_in, len_in = (sem(s) for s in (
        "cond_in", "bias_in", "router_in", "s4_in", "s4b_in", "len_in"))
    l1_in, ln_in, kz_in, kpad_in = (sem(s) for s in ("l1_in", "ln_in", "kz_in", "kpad_in"))
    toep_in = [sem(f"toep_in{g}") for g in range(4)]
    up_in, dn_in = sem("up_in"), sem("dn_in")
    out_sem = sem("out_sem")
    IDENT, TRI, PLACES, ORDER = range(1, 5)
    const_ok = sem("const_ok")
    mixr_done, xst_ok, msk_ok, rank_done, rank_ok, hot_ok, tok_done, tok_ok, eji_ok, bex_ok = (
        sem(s) for s in ("mixr_done", "xst_ok", "msk_ok", "rank_done", "rank_ok", "hot_ok",
                         "tok_done", "tok_ok", "eji_ok", "bex_ok"))
    bexl_ok = sem("bexl_ok")
    bx_done, bxh_ok, bxl_ok, w12h_ok, w12l_ok, w3h_ok, w3l_ok, bh_done, bsil_ok, bhid_ok, bt_done, bhh_ok, bhl_ok = (
        sem(s) for s in ("bx_done", "bxh_ok", "bxl_ok", "w12h_ok", "w12l_ok", "w3h_ok", "w3l_ok", "bh_done",
                         "bsil_ok", "bhid_ok", "bt_done", "bhh_ok", "bhl_ok"))
    by_done, yout_ok, comb_ok = sem("by_done"), sem("yout_ok"), sem("comb_ok")
    pool_step, vec_step = sem("pool_step"), sem("vec_step")
    cidx_ok, wbd_ok, mix_done, ah_ok, al_ok = (sem(s) for s in ("cidx_ok", "wbd_ok", "mix_done", "ah_ok", "al_ok"))
    rw_ok, gw_ok, tr_done, spar_ok, lg_done = (sem(s) for s in ("rw_ok", "gw_ok", "tr_done", "spar_ok", "lg_done"))
    a_done, c_done, y_done = sem("a_done"), sem("c_done"), sem("y_done")
    silu_ok, hid_ok, hidh_ok, hidl_ok, y_added = (sem(s) for s in ("silu_ok", "hid_ok", "hidh_ok", "hidl_ok", "y_added"))
    soft_in, soft_out, gates_ok, gt_done, gt_ok = (sem(s) for s in (
        "soft_in", "soft_out", "gates_ok", "gt_done", "gt_ok"))
    exps_ok, s4p_ok, s4a_ok, s4v_ok, lhs_ok, k_done, kout_ok, mask_ok = (sem(s) for s in (
        "exps_ok", "s4p_ok", "s4a_ok", "s4v_ok", "lhs_ok", "k_done", "kout_ok", "mask_ok"))
    cpart_ok, lenf_ok, stage_ok, b3z_ok = (sem(s) for s in (
        "cpart_ok", "lenf_ok", "stage_ok", "b3z_ok"))
    dim_ok, warm_ok, before_ok = sem("dim_ok"), sem("warm_ok"), sem("before_ok")
    arev_ok, b12_ok, ewt_ok = sem("arev_ok"), sem("b12_ok"), sem("ewt_ok")
    xt_done, u_ok, conv_done, y_ok, yh_ok, yl_ok, uph_ok, upl_ok = (sem(s) for s in (
        "xt_done", "u_ok", "conv_done", "y_ok", "yh_ok", "yl_ok", "uph_ok", "upl_ok"))
    dnh_ok, dnl_ok, fch_ok, fcl_ok, m2_done, m2h_ok, m2l_ok, resid_ok = (sem(s) for s in (
        "dnh_ok", "dnl_ok", "fch_ok", "fcl_ok", "m2_done", "m2h_ok", "m2l_ok", "resid_ok"))
    DECAY, TURNS, ANGLE = 1, 2, 3
    PART_1, PART_2, EXPS, SINE = 1, 2, 3, 4
    DIM_HI, RECIP, CLAMPED = 1, 2, 3
    lgt_done, lgt_ok = (sem(s) for s in ("lgt_done", "lgt_ok"))
    top_ok, rsc_ok, up_done, rel_ok, sq_ok, sqh_ok, sql_ok = (sem(s) for s in (
        "top_ok", "rsc_ok", "up_done", "rel_ok", "sq_ok", "sqh_ok", "sql_ok"))
    dn_done, lat_done, lath_ok, latl_ok, rt_done, latf_ok, rscb_done, rscb_ok, var_ok = (sem(s) for s in (
        "dn_done", "lat_done", "lath_ok", "latl_ok", "rt_done", "latf_ok", "rscb_done", "rscb_ok", "var_ok"))
    std_ok, nmr_ok, norm_ok, fin_ok = (sem(s) for s in ("std_ok", "nmr_ok", "norm_ok", "fin_ok"))

    def wait(eng, s, v):
        if isinstance(v, int) and v <= 0:
            return
        eng.wait_ge(s, v)

    def f(ap):
        return ap.bitcast(F32)

    xf = x.rearrange("b c t -> (b c) t")
    of = out.rearrange("b c t -> (b c) t")
    LOOPS = ((1, 3), (3, 4), (4, 5), (5, 7))
    W12 = slice(0, 2 * KC * P)
    W3 = slice(2 * KC * P, WCOLS)

    def group(i):
        return ((i * 4 - 1, 1, i * 2 - 1, 3, i - 1), (i * 4, 0, i * 2, 0, i), (i * 4 + 1, 1, i * 2, 1, i),
                (i * 4 + 2, 0, i * 2 + 1, 2, i))

    FIRST_BLOCKS = group(0)[1:]
    LAST_BLOCKS = group(7)

    def raw(s):
        return wraw[:, s, :] if s < 2 else wrawx[:, s - 2, :]

    def brow(s):
        return browa[:, s] if s < 2 else browb[:, s - 2]

    def split3(pe, dst, lhs, rhs, n_k, start=True, stop=True):
        for k in range(n_k):
            (lh, ll), (rh, rl) = lhs(k), rhs(k)
            pe.matmul(dst, lh, rh, start=(start and k == 0), stop=False)
            pe.matmul(dst, lh, rl, start=False, stop=False)
            mm = pe.matmul(dst, ll, rh, start=False, stop=(stop and k == n_k - 1))
        return mm

    block = ctx.enter_context(nc.Block())

    @block.sync
    def _(sp):
        def load_shared(part, s):
            cols = slice(part * P, (part + 1) * P)
            sp.dma_start(raw(s)[:, 0:KC * P].rearrange("p (k m) -> p k m", k=KC),
                         sw1[:, cols].rearrange("(k p) m -> p k m", p=P)).then_inc(sraw_in, 16)
            sp.dma_start(raw(s)[:, KC * P:2 * KC * P].rearrange("p (k m) -> p k m", k=KC),
                         sw2[:, cols].rearrange("(k p) m -> p k m", p=P)).then_inc(sraw_in, 16)
            sp.dma_start(raw(s)[:, W3], sw3[cols, :]).then_inc(sraw_in, 16)

        sp.dma_start(condb[:, :], bass.AP(tensor=cond.tensor, offset=0, ap=[[0, P], [1, B]])).then_inc(cond_in, 16)
        sp.dma_start(leni[:, :], bass.AP(tensor=length.tensor, offset=0, ap=[[0, P], [1, B]])).then_inc(len_in, 16)
        for j in range(4):
            sp.dma_start(acc[:, 2 * j:2 * j + 2, :],
                         xf[2 * j * P:(2 * j + 2) * P, :].rearrange("(i p) t -> p i t", p=P)).then_inc(x_in[j], 16)
        load_shared(0, 1)
        for k, (sb_, eb_) in enumerate(((sb1, eb1), (sb2, eb2))):
            sp.dma_start(bstage[0:SH, k, :], sb_.rearrange("(s p) -> s p", p=P)).then_inc(bias_in, 16)
            sp.dma_start(bstage[SH:G, k, :], eb_).then_inc(bias_in, 16)
        sp.dma_start(ewraw[:, :, :], expert_w.rearrange("(a p) m -> p a m", p=P)).then_inc(l1_in, 16)
        sp.dma_start(gwraw[:, :, :], gate_w.rearrange("(k p) e -> p k e", p=P)).then_inc(l1_in, 16)
        sp.wait_ge(b3z_ok, 1)
        sp.dma_start(b3m[0:1, :], sb3.rearrange("(o n) -> o n", o=1)).then_inc(l1_in, 16)
        sp.dma_start(b3m[SH:G, :], eb3).then_inc(l1_in, 16)
        sp.dma_start(drow[:, :], d_param.rearrange("(o n) -> o n", o=1)).then_inc(l1_in, 16)
        sp.dma_start(fcraw[:, :, :], fc1_w.rearrange("(k p) l -> p k l", p=P)).then_inc(l1_in, 16)
        sp.dma_start(fc2raw[:, :, :], fc2_w.rearrange("(a p) n -> p a n", p=P)).then_inc(l1_in, 16)

        def load_block(j, s):
            e = sp.value_load(eji[0:1, bass.ds(j, 1)], min_val=0, max_val=E - 1)
            for src, dst in ((ew1, 0), (ew2, KC * P)):
                sp.dma_start(raw(s)[:, dst:dst + KC * P].rearrange("p (k m) -> p k m", k=KC),
                             src[bass.ds(e, 1)].rearrange("o (k p) m -> p (o k) m", p=P)).then_inc(raw_in[s], 16)
            sp.dma_start(raw(s)[:, W3], ew3[bass.ds(e, 1)].rearrange("o p n -> (o p) n")).then_inc(raw_in[s], 16)
            sp.dma_start(brow(s).bitcast(F32), bsplit[bass.ds(e, 1)].bitcast(F32)).then_inc(raw_in[s], 16)

        def y_to_dram(j, par):
            sp.wait_ge(yout_ok, j + 1)
            sp.dma_start(ysort[bass.ds(j * P, P), :], yout[:, par, :]).then_inc(ys_out[par], 16)

        sp.wait_ge(eji_ok, 1)
        sp.wait_ge(bsplit_out, 32)
        load_block(0, 0)
        sp.wait_ge(swl_ok, 1)
        load_block(1, 1)
        sp.wait_ge(tr_done, 2)
        sp.wait_ge(eji_ok, 2)
        for s in range(2, RAWS):
            load_block(s, s)

        def step(j, par, s, load=True):
            if load:
                sp.wait_ge(w12l_ok, j + 1)
                sp.wait_ge(w3l_ok, j + 1)
                sp.wait_ge(bh_done, j + 1)
                load_block(j + RAWS, s)
            if not (isinstance(j, int) and j == 0):
                y_to_dram(j - 1, 1 - par)

        for j, par, m, s, ms in FIRST_BLOCKS:
            step(j, par, s)
        for lo, hi in LOOPS:
            with sp.Fori(lo, hi) as i:
                for j, par, m, s, ms in group(i):
                    step(j, par, s)
        def toeplitz(dst, h0, n, g):
            sp.dma_start(toep[:, dst:dst + n, :],
                         bass.AP(tensor=kpad.tensor, offset=h0 * PAD + 1, ap=[[1, P], [PAD, n], [1, T]]))\
                .then_inc(toep_in[g], 16)

        assert TS // 3 == 2 * RAWS
        for j, par, m, s, ms in LAST_BLOCKS:
            if s == 3:
                sp.wait_ge(w12l_ok, j + 1)
                sp.wait_ge(w3l_ok, j + 1)
                load_shared(1, s)
                sp.wait_ge(kz_in, 16)
                sp.wait_ge(kpad_in, 16)
            toeplitz(2 * s, 2 * s, 2, 0)
            step(j, par, s, load=False)
        y_to_dram(NB - 1, (NB - 1) % 2)

        for g in range(1, 3):
            sp.wait_ge(comb_ok, YS + 1)
            toeplitz(g * TS // 3, g * TS // 3, TS // 3, g)
        sp.wait_ge(swl_ok, 2)
        sp.wait_ge(tr_done, 3)
        sp.dma_start(upraw[:, :, :], up_w.rearrange("(k p) m -> p k m", p=P)).then_inc(up_in, 16)
        sp.wait_ge(y_added, 16)
        for dst, src in ((gam, ln_gamma), (bet, ln_beta)):
            sp.dma_start(dst[:, :], bass.AP(tensor=src.tensor, offset=0, ap=[[0, P], [1, T]])).then_inc(ln_in, 16)
        sp.wait_ge(comb_ok, K * NT)
        sp.dma_start(dnraw[:, :, :], down_w.rearrange("(j p) n -> p j n", p=P)).then_inc(dn_in, 16)
        wait(sp, conv_done, C - TS)
        toeplitz(0, TS, C - TS, 3)
        for i in range(NT):
            sp.wait_ge(fin_ok, i + 1)
            sp.dma_start(of[i * P:(i + 1) * P, :], acc[:, i, :]).then_inc(out_sem, 16)
        sp.wait_ge(out_sem, 16 * NT)

    @block.gpsimd
    def _(pool):
        steps = [0]

        def link(ins):
            steps[0] += 1
            ins.then_inc(pool_step, 1)
            pool.wait_ge(pool_step, steps[0])

        pool.iota(cpart[:, :], pattern=[[0, NT]], base=0, channel_multiplier=1).then_inc(cpart_ok, 1)
        pool.wait_ge(cidx_ok, 1)
        for i in range(NT):
            pool.indirect_dma_start(wsel[:, i, :], None, cond_w.rearrange("k c d -> (k c) d"),
                                    bass.IndirectOffsetOnAxis(ap=cidx[:, i:i + 1].bitcast(U32), axis=0))\
                .then_inc(wsel_in[int(i >= 2)], 16)
        link(pool.memset(ident[:, :], 0.0))
        pool.affine_select(out=ident[:, :], in_=ident[:, :], compare_op=ALU.not_equal, fill=1.0, base=0,
                           pattern=[[-1, P]], channel_multiplier=1).then_inc(const_ok, 1)
        link(pool.memset(ones[:, :], 1.0))
        link(pool.tensor_copy(onesr[:, :], ones[0:1, :]))
        pool.affine_select(out=tri[:, :], in_=ones[:, :], compare_op=ALU.is_gt, fill=0.0, base=0,
                           pattern=[[1, P]], channel_multiplier=-1).then_inc(const_ok, 1)
        pool.wait_ge(s4_in, 64)
        link(pool.tensor_copy(sstage[:, 2, 0:HN], cstage[:, :, 0]))
        link(pool.tensor_copy(sstage[:, 2, HN:P], cstage[:, :, 0]))
        link(pool.tensor_copy(sstage[:, 3, 0:HN], cstage[:, :, 1]))
        pool.tensor_copy(sstage[:, 3, HN:P], cstage[:, :, 1]).then_inc(stage_ok, 1)
        link(pool.iota(prow[:, :].bitcast(I32), pattern=[[1, P]], base=0, channel_multiplier=0))
        link(pool.tensor_copy(prow[:, :], prow[:, :].bitcast(I32)))
        link(pool.iota(tokf[:, :].bitcast(I32), pattern=[[P, NT]], base=0, channel_multiplier=1))
        pool.tensor_copy(tokf[:, :], tokf[:, :].bitcast(I32)).then_inc(const_ok, 1)
        link(pool.iota(tposi[:, 0, :], pattern=[[P, KC]], base=0, channel_multiplier=1))
        link(pool.iota(tposi[:, 1, :], pattern=[[P, KC]], base=P - 1, channel_multiplier=-1))
        link(pool.tensor_copy(tpos[:, :, :], tposi[:, :, :]))
        link(pool.iota(desci[:, :], pattern=[[-1, E]], base=E, channel_multiplier=0))
        pool.tensor_copy(desc[:, :], desci[:, :]).then_inc(const_ok, 1)
        link(pool.iota(lvali[:, 0:2 * LI], pattern=[[0, 2], [LJ, LI]], base=0, channel_multiplier=0))
        link(pool.iota(lvali[:, 2 * LI:2 * LI + LJ], pattern=[[1, LJ]], base=0, channel_multiplier=0))
        link(pool.iota(lvali[:, NL - 2:NL], pattern=[[0, 2]], base=1, channel_multiplier=0))
        link(pool.tensor_copy(lvals[:, :], lvali[:, :]))
        link(pool.tensor_scalar(lturn[:, :], lvals[:, :], 1 / (2 * math.pi), None, ALU.mult))
        for row in range(2):
            ps = slice(row * HN, (row + 1) * HN)
            for a, b, v in ((0, LI, row), (LI, 2 * LI, row + 1), (2 * LI, 2 * LI + LJ, 1 - row),
                            (NL - 2, NL - 1, 0), (NL - 1, NL, 1)):
                link(pool.memset(shq[ps, a:b], v / 4))
        link(pool.tensor_scalar(shr[:, :], shq[:, :], 2 * math.pi, None, ALU.mult))
        link(pool.memset(epst[:, :], LN_EPS))
        pool.wait_ge(len_in, 16)
        pool.tensor_copy(lenf[:, :], leni[:, :]).then_inc(lenf_ok, 1)
        link(pool.memset(zrow[:, :], 0.0))
        pool.dma_start(kpad[:, 0:P], zrow[:, :]).then_inc(kz_in, 16)

        EA, DT, DRE, DIM, DLO, DEN, RDEN, NR, QR, QI, X1, X2, CR2, CI2 = range(14)
        w = [sw[:, k, :] for k in range(14)]
        pool.wait_ge(exps_ok, 2)
        link(pool.tensor_tensor(w[DRE], w[EA], w[DT], ALU.mult))
        link(pool.tensor_tensor(w[DIM], spar[:, 1, :], w[DT], ALU.mult))
        link(pool.tensor_tensor(w[X1], w[EA], w[EA], ALU.mult))
        link(pool.tensor_tensor(w[X2], spar[:, 1, :], spar[:, 1, :], ALU.mult))
        link(pool.tensor_tensor(w[DEN], w[X1], w[X2], ALU.add))
        pool.tensor_copy(w[X1], w[DIM]).then_inc(dim_ok, 1)

        def cols(ap):
            return ap.unsqueeze(2).broadcast_to([P, C, NL])

        def heads(ap):
            return ap.unsqueeze(1).broadcast_to([P, C, NL])

        pool.tensor_tensor(decay[:, :, :], cols(w[DRE]), heads(lvals[:, :]), ALU.mult).then_inc(s4p_ok, 1)
        link(pool.tensor_tensor(turns[:, :, :], cols(w[DIM]), heads(lturn[:, :]), ALU.mult))
        link(pool.tensor_tensor(turns[:, :, :], turns[:, :, :], heads(shq[:, :]), ALU.add))
        pool.tensor_scalar(turns[:, :, :], turns[:, :, :], MAGIC, -MAGIC, ALU.add, ALU.add).then_inc(s4p_ok, 1)
        pool.wait_ge(s4v_ok, DIM_HI)
        link(pool.tensor_tensor(w[DLO], w[DIM], f(dimh[:, :]), ALU.subtract))
        link(pool.tensor_tensor(angle[:, :, :], cols(f(dimh[:, :])), heads(lvals[:, :]), ALU.mult))
        pool.wait_ge(s4a_ok, PART_1)
        link(pool.tensor_tensor(angle[:, :, :], angle[:, :, :], term[:, :, :], ALU.subtract))
        link(pool.tensor_tensor(term[:, :, :], cols(w[DLO]), heads(lvals[:, :]), ALU.mult))

        def gather(j):
            wait(pool, bx_done, j - RAWS + 1)
            pool.indirect_dma_start(xg[:, j % RAWS, :], None, xrow,
                                    bass.IndirectOffsetOnAxis(ap=tokx[:, j:j + 1].bitcast(U32), axis=0))\
                .then_inc(xg_in[j % RAWS], 16)

        pool.wait_ge(tok_ok, 1)
        for par in range(2):
            pool.wait_ge(xrow_out[par], 16 * NT // 4)
        gather(0)
        gather(1)
        pool.wait_ge(s4a_ok, PART_2)
        link(pool.tensor_tensor(angle[:, :, :], angle[:, :, :], turns[:, :, :], ALU.subtract))
        gather(2)
        gather(3)
        link(pool.tensor_tensor(angle[:, :, :], angle[:, :, :], term[:, :, :], ALU.add))
        gather(4)
        pool.tensor_tensor(angle[:, :, :], angle[:, :, :], heads(shr[:, :]), ALU.add).then_inc(s4p_ok, 1)
        for j in range(5, 18):
            gather(j)
        pool.wait_ge(s4a_ok, SINE)
        link(pool.tensor_tensor(term[:, :, :], decay[:, :, :], angle[:, :, :], ALU.mult))
        gather(18)
        pool.wait_ge(s4v_ok, RECIP)
        er, ei = term[:, :, NL - 1], term[:, :, NL - 2]
        link(pool.tensor_scalar(w[NR], er, -1.0, None, ALU.add))
        link(pool.tensor_tensor(w[X1], ei, spar[:, 1, :], ALU.mult))
        link(pool.tensor_tensor(w[X2], w[NR], w[EA], ALU.mult))
        link(pool.tensor_tensor(w[X1], w[X1], w[X2], ALU.subtract))
        link(pool.tensor_tensor(w[QR], w[X1], w[RDEN], ALU.mult))
        link(pool.tensor_tensor(w[X1], w[NR], spar[:, 1, :], ALU.mult))
        link(pool.tensor_tensor(w[X2], ei, w[EA], ALU.mult))
        link(pool.tensor_tensor(w[X1], w[X1], w[X2], ALU.add))
        link(pool.tensor_tensor(w[X1], w[X1], w[RDEN], ALU.mult))
        link(pool.tensor_scalar(w[QI], w[X1], -1.0, None, ALU.mult))
        gather(19)
        for dst, a, b, op in ((CR2, QR, QI, ALU.subtract), (CI2, QI, QR, ALU.add)):
            link(pool.tensor_tensor(w[X1], spar[:, 2, :], w[a], ALU.mult))
            link(pool.tensor_tensor(w[X2], spar[:, 3, :], w[b], ALU.mult))
            link(pool.tensor_tensor(w[X1], w[X1], w[X2], op))
            link(pool.tensor_scalar(w[dst], w[X1], 2.0, None, ALU.mult))

        def ncols(ap):
            return ap.unsqueeze(2).broadcast_to([P, C, LI])

        gather(20)
        link(pool.tensor_tensor(lhs_k[:, :, :], term[:, :, LI:2 * LI], ncols(w[CR2]), ALU.mult))
        link(pool.tensor_tensor(tmp_k[:, :, :], term[:, :, 0:LI], ncols(w[CI2]), ALU.mult))
        gather(21)
        pool.tensor_tensor(lhs_k[:, :, :], lhs_k[:, :, :], tmp_k[:, :, :], ALU.subtract).then_inc(lhs_ok, 1)
        for j in range(22, 24):
            gather(j)

        pool.wait_ge(kout_ok, 2)
        link(pool.tensor_tensor(kout[0:1, :, 0], kout[0:1, :, 0], drow[:, :], ALU.add))
        pool.dma_start(kpad[:, P:PAD].rearrange("h (i j) -> i h j", i=LI), kout[:, :, :]).then_inc(kpad_in, 16)
        for j in range(24, NB):
            gather(j)

        pool.wait_ge(ys_out[0], 16 * ((NB + 1) // 2))
        pool.wait_ge(ys_out[1], 16 * (NB // 2))
        for n in range(K * NT):
            i, k = n // K, n % K
            wait(pool, comb_ok, n - YS + 1)
            pool.indirect_dma_start(yg[:, n % YS, :], None, ysort,
                                    bass.IndirectOffsetOnAxis(ap=sloti[:, k, i:i + 1].bitcast(U32), axis=0))\
                .then_inc(yg_in[n % YS], 16)
        pool.wait_ge(ln_in, 32)
        for i in range(NT):
            pool.wait_ge(xt_done, i + 1)
            pool.tensor_tensor(acc[:, i, :], acc[:, i, :], bet[:, :], ALU.add).then_inc(resid_ok, 1)
        for j in range(JC):
            pool.wait_ge(dnh_ok, j + 1)
            pool.tensor_tensor(dnl[:, j, :], dnraw[:, j, :], f(dnh[:, j, :]), ALU.subtract).then_inc(dnl_ok, 1)
        pool.wait_ge(fch_ok, 1)
        pool.tensor_tensor(fcl[:, :, :], fcraw[:, :, :], f(fch[:, :, :]), ALU.subtract).then_inc(fcl_ok, 1)

    @block.scalar
    def _(act):
        def bcast(src, n):
            return bass.AP(tensor=src.tensor, offset=0, ap=[[0, P], [1, n]])

        for half in range(2):
            act.dma_start(sstage[:, 0, half * HN:(half + 1) * HN], log_a_real).then_inc(s4_in, 16)
        act.dma_start(cstage[:, :, :], c_param).then_inc(s4_in, 16)
        act.dma_start(sdt[:, :], bcast(log_dt, C)).then_inc(s4_in, 16)
        for half in range(2):
            act.dma_start(sstage[:, 1, half * HN:(half + 1) * HN], a_imag).then_inc(s4b_in, 16)
        act.dma_start(rwraw[:, :, :], router_w.rearrange("(k p) e -> p k e", p=P)).then_inc(router_in, 16)
        act.dma_start(rb[:, 0, :], bcast(router_b, E)).then_inc(router_in, 16)
        act.dma_start(rb[:, 1, :], bcast(router_bias, E)).then_inc(router_in, 16)
        for k, eb_ in enumerate((eb1, eb2)):
            act.dma_start(bexp[:, k * P:(k + 1) * P], eb_).then_inc(bexp_in, 16)

        def x_row(i):
            if i % 2 == 0:
                wait(act, xrow_out[i // 2 % 2], 16 * (i // 4))
            act.wait_ge(mixr_done, i + 1)
            wait(act, mix_done, i - 3)
            act.activation(xstage[:, i % 4, :], bank[(2 * i + 1) % 8][:, :], ACT.Copy).then_inc(xst_ok, 1)
            if i % 2:
                act.wait_ge(xst_ok, i + 1)
                act.dma_start(xrow[(i - 1) * P:(i + 1) * P, :].rearrange("(i p) t -> p i t", p=P),
                              xstage[:, i % 4 - 1:i % 4 + 1, :]).then_inc(xrow_out[i // 2 % 2], 16)

        x_row(0)
        for i in range(NT):
            if i + 1 < NT:
                x_row(i + 1)
            if i == 0:
                act.wait_ge(router_in, 48)
                act.activation(rwc[:, :, 0:E], rwraw[:, :, :], ACT.Copy).then_inc(rw_ok, 1)
                act.wait_ge(bexp_in, 32)
                act.activation(bexh[:, :], bexp[:, :], ACT.Copy).then_inc(bex_ok, 1)
                act.wait_ge(s4_in, 64)
                act.activation(sw[:, 1, :], sdt[:, :], ACT.Exp).then_inc(exps_ok, 1)
            if i == 1:
                act.wait_ge(tr_done, 1)
                act.activation(spar[:, :, :], bank[7][:, 0:4 * C].rearrange("p (k h) -> p k h", k=4), ACT.Copy)\
                    .then_inc(spar_ok, 1)
                act.wait_ge(spar_ok, 1)
                act.activation(sw[:, 0, :], spar[:, 0, :], ACT.Exp).then_inc(exps_ok, 1)
            act.wait_ge(mix_done, i + 1)
            act.activation(ah[:, :, i * P:(i + 1) * P], bank[2 * i % 8][:, :].rearrange("p (k n) -> p k n", k=KC), ACT.Copy)\
                .then_inc(ah_ok, 1)

        def split_hi(part, s):
            act.wait_ge(sraw_in, 48 * (part + 1))
            act.activation(whi[:, 1, :], raw(s), ACT.Copy).then_inc(swh_ok, 1)

        for q in range(2):
            act.wait_ge(lgt_done, q + 1)
            act.activation(ltr[:, q, :], bank[q][0:2 * E, :], ACT.Copy).then_inc(lgt_ok, 1)
        split_hi(0, 1)
        act.wait_ge(soft_in, 1)
        act.activation(w1t[:, :, :], w1t[:, :, :], ACT.Exp).then_inc(soft_out, 1)
        act.wait_ge(s4p_ok, TURNS)
        act.activation(term[:, :, :], turns[:, :, :], ACT.Copy, scale=PI_1).then_inc(s4a_ok, 1)
        act.wait_ge(s4a_ok, PART_1)
        act.activation(turns[:, :, :], turns[:, :, :], ACT.Copy, scale=PI_2).then_inc(s4a_ok, 1)
        act.wait_ge(s4p_ok, DECAY)
        act.activation(decay[:, :, :], decay[:, :, :], ACT.Exp, scale=-1.0).then_inc(s4a_ok, 1)
        act.wait_ge(bexl_ok, 1)
        act.dma_start(bsplit[:, 0, :].bitcast(F32), bexh[:, :].bitcast(F32)).then_inc(bsplit_out, 16)
        act.dma_start(bsplit[:, 1, :].bitcast(F32), bexl[:, :].bitcast(F32)).then_inc(bsplit_out, 16)

        def shared_silu(u):
            act.wait_ge(a_done, u + 1)
            wait(act, hid_ok, u - 1)
            act.activation(silu[:, u % 2, :], bank[4 + u % 2][:, :], ACT.Silu, bias=b12[:, 0, u // 2:u // 2 + 1])\
                .then_inc(silu_ok, 1)

        def shared_hi(u):
            act.wait_ge(hid_ok, u + 1)
            wait(act, y_done, (u - 1) * 4)
            act.activation(hidh[:, u % 2, :], hid[:, u % 2, :], ACT.Copy).then_inc(hidh_ok, 1)

        act.wait_ge(b12_ok, 1)
        for par in range(2):
            act.wait_ge(xrow_out[par], 16 * NT // 4)
        for u in range(2):
            shared_silu(u)
        for u in range(2):
            shared_hi(u)

        def w12_hi(n, par, s, ms):
            act.wait_ge(raw_in[s], ms * 64 + 64)
            wait(act, bh_done, n - 1)
            act.activation(whi[:, par, W12], raw(s)[:, W12], ACT.Copy).then_inc(w12h_ok, 1)

        def x_hi(n, par):
            act.wait_ge(bx_done, n + 1)
            wait(act, bh_done, n - 1)
            act.activation(xth[:, par, :, :], bank[par][:, :].rearrange("p (k n) -> p k n", k=KC), ACT.Copy)\
                .then_inc(bxh_ok, 1)

        def y_out(n, par, m):
            act.wait_ge(by_done, n + 1)
            wait(act, ys_out[par], m * 16)
            act.activation(yout[:, par, :], bank[6 + par][:, :], ACT.Copy).then_inc(yout_ok, 1)

        def step(j, par, m, s, ms, load=True, ahead=True):
            act.wait_ge(bh_done, j + 1)
            wait(act, bhid_ok, j - 1)
            act.activation(bsil[:, par, :], bank[2 + par][:, 0:P], ACT.Silu).then_inc(bsil_ok, 1)
            wait(act, by_done, j - 1)
            act.activation(whi[:, par, W3], raw(s)[:, W3], ACT.Copy).then_inc(w3h_ok, 1)
            if not (isinstance(j, int) and j == 0):
                y_out(j - 1, 1 - par, m + par - 1)
            if ahead:
                x_hi(j + 2, par)
            act.wait_ge(bt_done, j + 1)
            wait(act, by_done, j - 1)
            act.activation(bhh[:, par, :], bank[2 + par][:, 2 * P:3 * P], ACT.Copy).then_inc(bhh_ok, 1)
            if load:
                w12_hi(j + 2, par, (s + 2) % RAWS, ms + (s + 2) // RAWS)

        w12_hi(0, 0, 0, 0)
        x_hi(0, 0)
        act.wait_ge(y_done, 8)
        w12_hi(1, 1, 1, 0)
        x_hi(1, 1)
        for blk_ in FIRST_BLOCKS:
            step(*blk_)
        for n, (lo, hi) in enumerate(LOOPS):
            with act.Fori(lo, hi) as i:
                for blk_ in group(i):
                    step(*blk_)
            if n == 1:
                act.wait_ge(s4v_ok, CLAMPED)
                act.activation(angle[:, :, :], angle[:, :, :], ACT.Sin).then_inc(s4a_ok, 1)
            if n == 2:
                act.wait_ge(tr_done, 3)
                act.activation(ewt[:, :, :], bank[4][:, 0:LC * LAT].rearrange("p (a l) -> p a l", a=LC), ACT.Copy)\
                    .then_inc(ewt_ok, 1)
                for j in (1, 0):
                    act.wait_ge(k_done, 2 - j)
                    act.activation(kout[:, j * 16:(j + 1) * 16, :],
                                   bank[4 + j][0:LI, :].rearrange("p (h j) -> p h j", j=LJ), ACT.Copy)\
                        .then_inc(kout_ok, 1)
        for blk_ in LAST_BLOCKS:
            step(*blk_, load=(blk_[0] + 2 < NB), ahead=(blk_[0] + 2 < NB))
        wait(act, by_done, NB - 1)
        split_hi(1, 3)
        y_out(NB - 1, (NB - 1) % 2, (NB - 1) // 2)

        for j in range(2):
            act.wait_ge(gt_done, j + 1)
            act.activation(gt[:, j * HALF:(j + 1) * HALF], bank[4 + j][0:G, :], ACT.Copy).then_inc(gt_ok, 1)
        act.wait_ge(l1_in, 16 * 7)
        act.activation(gwc[:, :, 0:NE1], gwraw[:, :, :], ACT.Copy).then_inc(gw_ok, 1)
        for u in range(2, 4):
            shared_silu(u)
            shared_hi(u)

        for i in range(NT):
            act.wait_ge(comb_ok, K * (i + 1))
            act.wait_ge(y_added, 2 * TH + i + 1)
            wait(act, xt_done, i - 1)
            act.activation(arev[:, i % 2, :], acc[:, i, ::-1], ACT.Copy).then_inc(arev_ok, 1)
        act.wait_ge(up_in, 16)
        act.wait_ge(y_done, 16)
        act.wait_ge(xt_done, NT)
        for k in range(KC):
            act.activation(uph[:, k, :], upraw[:, k, :], ACT.Copy).then_inc(uph_ok, 1)
        for g in range(C // 4):
            act.wait_ge(y_ok, g + 1)
            act.activation(ah[:, :, :].rearrange("p k (b h) -> p h k b", h=C)[:, 4 * g:4 * g + 4],
                           ycv[:, g % 2, :, :].rearrange("p h (k b) -> p h k b", k=KC), ACT.Copy).then_inc(yh_ok, 1)
            if g >= C // 4 - 2:
                act.wait_ge(conv_done, TS)
                act.wait_ge(dn_in, 16)
                for j in range((g - C // 4 + 2) * JC // 2, (g - C // 4 + 3) * JC // 2):
                    act.activation(dnh[:, j, :], dnraw[:, j, :], ACT.Copy).then_inc(dnh_ok, 1)
        for q in range(2):
            act.wait_ge(lgt_done, 2 + q + 1)
            act.activation(ltg[:, q, :], bank[q][0:2 * NE1, :], ACT.Copy).then_inc(lgt_ok, 1)
        for a in range(LC):
            act.wait_ge(m2_done, a + 1)
            act.activation(m2h[:, a, :], bank[6 + a][:, :], ACT.Copy).then_inc(m2h_ok, 1)
        act.activation(fch[:, :, :], fcraw[:, :, :], ACT.Copy).then_inc(fch_ok, 1)

        def std_of(i):
            act.wait_ge(var_ok, i + 1)
            act.activation(std[:, i:i + 1], mv[:, i, 1:2], ACT.Sqrt, bias=epst[:, :]).then_inc(std_ok, 1)

        def normalize(i):
            act.wait_ge(nmr_ok, i + 1)
            wait(act, fin_ok, i - TH + 1)
            act.activation(osum[:, i % TH, :], bank[i % TH][:, :], ACT.Identity, scale=rstd[:, i:i + 1],
                           bias=nmr[:, i:i + 1]).then_inc(norm_ok, 1)

        for q in range(2):
            for j in range(JC):
                v = q * JC + j
                if v == 0:
                    act.wait_ge(upl_ok, KC)
                if v == JC - 2:
                    act.wait_ge(rscb_done, 1)
                    for k in range(2):
                        act.activation(rscb[:, k, :], bank[6 + k][:, :], ACT.Copy).then_inc(rscb_ok, 1)
                if j == JC - 1:
                    for a in range(LC):
                        act.wait_ge(latf_ok, LC * q + a + 1)
                        act.wait_ge(dnl_ok, JC)
                        wait(act, rt_done, q * TH)
                        act.activation(lath[:, a, :], latf[:, a, :], ACT.Copy).then_inc(lath_ok, 1)
                act.wait_ge(up_done, v + 1)
                wait(act, sq_ok, v - 1)
                act.activation(rel[:, v % 2, :], bank[4 + v % 2][:, :], ACT.Relu).then_inc(rel_ok, 1)
                act.wait_ge(sq_ok, v + 1)
                wait(act, dn_done, (v - 1) * TH)
                act.activation(sqh[:, v % 2, :], sq[:, v % 2, :], ACT.Copy).then_inc(sqh_ok, 1)
            if q == 0:
                std_of(0)
                std_of(1)
                for i in range(TH):
                    normalize(i)
                    if i + 2 < TH:
                        std_of(i + 2)
            else:
                for i in range(TH, NT):
                    std_of(i)
                    normalize(i)

    @block.vector
    def _(dve):
        steps = [0]

        def link(ins):
            steps[0] += 1
            ins.then_inc(vec_step, 1)
            dve.wait_ge(vec_step, steps[0])

        tt = dve.tensor_tensor
        dve.memset(warm[:, :], 0.0).then_inc(warm_ok, 1)
        dve.memset(gates[:, 0:SH, :], 1.0).then_inc(gates_ok, 1)
        dve.memset(b3m[:, :], 0.0).then_inc(b3z_ok, 1)
        link(dve.memset(wbd[:, :, :], 0.0))
        dve.wait_ge(cpart_ok, 1)
        link(dve.tensor_scalar(cpart[:, :], cpart[:, :], C - 1, None, ALU.bitwise_and))
        dve.wait_ge(cond_in, 16)
        for b in range(BT):
            s = slice(b * C, (b + 1) * C)
            link(dve.tensor_scalar(cidx[s, :], condb[s, b::BT], C, None, ALU.mult))
        tt(cidx[:, :], cidx[:, :], cpart[:, :], ALU.add).then_inc(cidx_ok, 1)
        for g, (lo, hi) in enumerate(((0, 2), (2, NT))):
            dve.wait_ge(wsel_in[g], 16 * (hi - lo))
            for b in range(BT):
                s = slice(b * C, (b + 1) * C)
                dve.tensor_copy(wbd[s, lo:hi, s], wsel[s, lo:hi, :]).then_inc(wbd_ok, 1)
        dve.wait_ge(const_ok, PLACES)
        tt(before[:, :, :], prow[:, 0:E].unsqueeze(1).broadcast_to([P, E, E]),
           prow[:, 0:E].unsqueeze(2).broadcast_to([P, E, E]), ALU.is_lt).then_inc(before_ok, 1)
        dve.wait_ge(before_ok, 1)
        dve.wait_ge(rw_ok, 1)
        tt(rwc[:, :, E:2 * E], rwraw[:, :, :], f(rwc[:, :, 0:E]), ALU.subtract).then_inc(rw_ok, 1)
        dve.wait_ge(bex_ok, 1)
        tt(bexl[:, :], bexp[:, :], f(bexh[:, :]), ALU.subtract).then_inc(bexl_ok, 1)
        for i in range(NT):
            dve.wait_ge(ah_ok, i + 1)
            tt(al[:, :, i * P:(i + 1) * P], bank[2 * i % 8][:, :].rearrange("p (k n) -> p k n", k=KC),
               f(ah[:, :, i * P:(i + 1) * P]), ALU.subtract).then_inc(al_ok, 1)

        dve.wait_ge(dim_ok, 1)
        dve.tensor_copy(dimh[:, :], sw[:, 3, :]).then_inc(s4v_ok, 1)
        dve.reciprocal(sw[:, 6, :], sw[:, 5, :]).then_inc(s4v_ok, 1)

        def split_lo(part, s):
            dve.wait_ge(swh_ok, part + 1)
            tt(wlo[:, 1, :], raw(s), f(whi[:, 1, :]), ALU.subtract).then_inc(swl_ok, 1)

        split_lo(0, 1)

        def tiles(ap, n):
            return ap.unsqueeze(2).broadcast_to([P, NT, n])

        def rows(ap, n):
            return ap.unsqueeze(1).broadcast_to([P, NT, n])

        dve.wait_ge(lg_done, 1)
        lgv = bank[2][:, 0:NT * 2 * E].rearrange("p (i r e) -> p i r e", r=2, e=E)
        link(tt(sc[:, :, :], lgv[:, :, 1, :], rows(rb[:, 0, :], E), ALU.add))
        link(tt(sc[:, :, :], lgv[:, :, 0, :], sc[:, :, :], ALU.add))

        def first_max(dst, src, tmp, n):
            link(dve.tensor_reduce(red[:, 0, :], src, AX.X, ALU.max))
            link(tt(tmp, src, tiles(red[:, 0, :], n), ALU.is_equal))
            link(tt(tmp, tmp, rows(desc[:, 0:n], n), ALU.mult))
            link(dve.tensor_reduce(red[:, 1, :], tmp, AX.X, ALU.max))
            link(tt(dst, tmp, tiles(red[:, 1, :], n), ALU.is_equal))

        link(dve.tensor_reduce(red[:, 0, :], sc[:, :, :], AX.X, ALU.max))
        tt(w1t[:, :, :], sc[:, :, :], tiles(red[:, 0, :], E), ALU.subtract).then_inc(soft_in, 1)
        dve.wait_ge(soft_out, 1)
        link(dve.tensor_reduce(red[:, 0, :], w1t[:, :, :], AX.X, ALU.add))
        link(dve.reciprocal(red[:, 1, :], red[:, 0, :]))
        link(tt(sc[:, :, :], w1t[:, :, :], tiles(red[:, 1, :], E), ALU.mult))
        link(tt(sc[:, :, :], sc[:, :, :], rows(rb[:, 1, :], E), ALU.add))
        link(dve.tensor_reduce(gm[:, :, :], sc[:, :, :].rearrange("p i (g e) -> p i g e", g=NG), AX.X, ALU.max))
        dve.wait_ge(const_ok, ORDER)
        first_max(oh[:, 0, :, 0:NG], gm[:, :, :], w1t[:, :, 0:NG], NG)
        link(dve.scalar_tensor_tensor(gm[:, :, :], oh[:, 0, :, 0:NG], -BIG, gm[:, :, :], ALU.mult, ALU.add))
        first_max(oh[:, 1, :, 0:NG], gm[:, :, :], w1t[:, :, 0:NG], NG)
        link(tt(keep[:, :, :], oh[:, 0, :, 0:NG], oh[:, 1, :, 0:NG], ALU.add))
        link(dve.tensor_scalar(keep[:, :, :], keep[:, :, :], -1.0, BIG, ALU.add, ALU.mult))
        link(tt(w2t[:, :, :].rearrange("p i (g e) -> p i g e", g=NG), sc[:, :, :].rearrange("p i (g e) -> p i g e", g=NG),
                keep[:, :, :].unsqueeze(3).broadcast_to([P, NT, NG, E // NG]), ALU.add))
        first_max(oh[:, 0, :, :], w2t[:, :, :], w1t[:, :, :], E)
        link(dve.scalar_tensor_tensor(w2t[:, :, :], oh[:, 0, :, :], -BIG, w2t[:, :, :], ALU.mult, ALU.add))
        first_max(oh[:, 1, :, :], w2t[:, :, :], w1t[:, :, :], E)
        tt(w2t[:, :, :], oh[:, 0, :, :], oh[:, 1, :, :], ALU.add).then_inc(msk_ok, 1)
        dve.wait_ge(msk_ok, 1)
        tt(gates[:, SH:G, :].rearrange("p e i -> p i e"), w2t[:, :, :], sc[:, :, :], ALU.mult).then_inc(gates_ok, 1)

        dve.wait_ge(tr_done, 2)
        dve.tensor_copy(b12[:, :, :], bank[3][:, 0:2 * G].rearrange("p (k g) -> p k g", k=2)).then_inc(b12_ok, 1)
        dve.wait_ge(b12_ok, 1)

        def add_y(uy, i):
            tile = uy % 2 * TH + i
            dve.wait_ge(y_done, uy * 4 + i + 1)
            wait(dve, y_added, uy * 4 + i - 7)
            tt(acc[:, tile, :], bank[i][:, :], acc[:, tile, :], ALU.add).then_inc(y_added, 1)

        def shared_hid(u):
            q, part = u % 2, u // 2
            dve.wait_ge(c_done, u + 1)
            dve.wait_ge(silu_ok, u + 1)
            wait(dve, hidh_ok, u - 1)
            wait(dve, hidl_ok, u - 1)
            dve.scalar_tensor_tensor(hid[:, q, :], bank[6 + q][:, :], b12[:, 1, part:part + 1],
                                     silu[:, q, :], ALU.add, ALU.mult).then_inc(hid_ok, 1)

        def shared_lo(u):
            dve.wait_ge(hidh_ok, u + 1)
            wait(dve, y_done, (u - 1) * 4)
            tt(hidl[:, u % 2, :], hid[:, u % 2, :], f(hidh[:, u % 2, :]), ALU.subtract).then_inc(hidl_ok, 1)

        dve.wait_ge(rank_done, 1)
        rk = bank[2][:, 0:NT * E].rearrange("p (i e) -> p i e", e=E)
        tot = bank[2][:, NT * E:2 * NT * E].rearrange("p (i e) -> p i e", e=E)
        link(dve.memset(pre[:, 0, :], 0.0))
        link(dve.tensor_copy(pre[:, 1, :], tot[:, 0, :]))
        for i in range(2, NT + 1):
            link(tt(pre[:, i, :], pre[:, i - 1, :], tot[:, i - 1, :], ALU.add))
        NBL, FIRST, END = range(3)
        b_ = [blk[:, n, :] for n in range(3)]
        link(dve.tensor_scalar(b_[NBL], pre[:, NT, :], 1 / P, (P - 1) / P - FLOOR, ALU.mult, ALU.add))
        link(dve.tensor_scalar(b_[NBL], b_[NBL], MAGIC, -MAGIC, ALU.add, ALU.add))
        link(tt(nbef[:, :, :], b_[NBL].unsqueeze(1).broadcast_to([P, E, E]), before[:, :, :], ALU.mult))
        link(dve.tensor_reduce(b_[FIRST], nbef[:, :, :], AX.X, ALU.add))
        link(tt(rank[:, :, :], rk, pre[:, 0:NT, :], ALU.add))
        dve.scalar_tensor_tensor(rank[:, :, :], rows(b_[FIRST], E), float(P), rank[:, :, :], ALU.mult, ALU.add)\
            .then_inc(rank_ok, 1)
        dve.wait_ge(rank_ok, 1)

        def picked(dst, src):
            link(tt(w12t[:, :, :, :], oh[:, :, :, :], src.unsqueeze(1).broadcast_to([P, K, NT, E]), ALU.mult))
            link(dve.tensor_reduce(dst.rearrange("p k i -> p (k i)"), w12t[:, :, :, :].rearrange("p k i e -> p (k i) e"),
                                   AX.X, ALU.add))

        picked(slot[:, :, :], rank[:, :, :])
        link(dve.tensor_scalar(sblk[:, :, :], slot[:, :, :], 1 / P, -FLOOR, ALU.mult, ALU.add))
        link(dve.tensor_scalar(sblk[:, :, :], sblk[:, :, :], MAGIC, -MAGIC, ALU.add, ALU.add))
        link(dve.scalar_tensor_tensor(srem[:, :, :], sblk[:, :, :], -float(P), slot[:, :, :], ALU.mult, ALU.add))

        def pairs(ap, n):
            return ap.rearrange("p k i -> p (k i)").unsqueeze(2).broadcast_to([P, K * NT, n])

        link(tt(hott[:, :, :], pairs(sblk[:, :, :], NSLOT),
                prow[:, 0:NSLOT].unsqueeze(1).broadcast_to([P, K * NT, NSLOT]), ALU.is_equal))
        for k in range(K):
            tt(hotb[:, k * NT:(k + 1) * NT, :], hott[:, k * NT:(k + 1) * NT, :],
               tokf[:, :].unsqueeze(2).broadcast_to([P, NT, NSLOT]), ALU.mult).then_inc(hot_ok, 1)
        for k in range(K):
            tt(hotp[:, k * NT:(k + 1) * NT, :], srem[:, k, :].unsqueeze(2).broadcast_to([P, NT, P]),
               prow[:, :].unsqueeze(1).broadcast_to([P, NT, P]), ALU.is_equal).then_inc(hot_ok, 1)
        link(tt(b_[END], b_[FIRST], b_[NBL], ALU.add))
        link(tt(cmp[:, :, :], blk[0:1, END, :].unsqueeze(1).broadcast_to([1, NSLOT, E]),
                prow[0:1, 0:NSLOT].unsqueeze(2).broadcast_to([1, NSLOT, E]), ALU.is_le))
        link(dve.tensor_reduce(ejf[:, :], cmp[:, :, :], AX.X, ALU.add))
        link(dve.tensor_scalar(ejf[:, :], ejf[:, :], E - 1.0, None, ALU.min))
        dve.tensor_copy(eji[:, :], ejf[:, :]).then_inc(eji_ok, 1)
        picked(gk[:, :, :], sc[:, :, :])
        dve.tensor_copy(sloti[:, :, :], slot[:, :, :]).then_inc(eji_ok, 1)
        shared_hid(0)
        shared_lo(0)
        dve.wait_ge(tok_done, 1)
        dve.tensor_copy(tokx[:, :], bank[3][:, 0:NSLOT]).then_inc(tok_ok, 1)
        shared_hid(1)
        shared_lo(1)
        for u in range(2):
            for i in range(TH):
                add_y(u, i)

        dve.wait_ge(lenf_ok, 1)
        tt(mask[:, :, :, :].rearrange("p r k b -> p (r k) b"), lenf[:, :].unsqueeze(1).broadcast_to([P, 2 * KC, B]),
           tpos[:, :, :].rearrange("p r k -> p (r k)").unsqueeze(2).broadcast_to([P, 2 * KC, B]), ALU.is_gt)\
            .then_inc(mask_ok, 1)

        def w12_lo(n, par, s):
            dve.wait_ge(w12h_ok, n + 1)
            wait(dve, bh_done, n - 1)
            tt(wlo[:, par, W12], raw(s)[:, W12], f(whi[:, par, W12]), ALU.subtract).then_inc(w12l_ok, 1)

        def x_lo(n, par):
            dve.wait_ge(bxh_ok, n + 1)
            wait(dve, bh_done, n - 1)
            tt(xtl[:, par, :, :], bank[par][:, :].rearrange("p (k n) -> p k n", k=KC), f(xth[:, par, :, :]),
               ALU.subtract).then_inc(bxl_ok, 1)

        def step(j, par, m, s, ms, ahead=True):
            dve.wait_ge(bsil_ok, j + 1)
            wait(dve, bt_done, j - 1)
            tt(bhid[:, par, :], bank[2 + par][:, P:2 * P], bsil[:, par, :], ALU.mult).then_inc(bhid_ok, 1)
            dve.wait_ge(w3h_ok, j + 1)
            wait(dve, by_done, j - 1)
            tt(wlo[:, par, W3], raw(s)[:, W3], f(whi[:, par, W3]), ALU.subtract).then_inc(w3l_ok, 1)
            if ahead:
                x_lo(j + 2, par)
            dve.wait_ge(bhh_ok, j + 1)
            wait(dve, by_done, j - 1)
            tt(bhl[:, par, :], bank[2 + par][:, 2 * P:3 * P], f(bhh[:, par, :]), ALU.subtract).then_inc(bhl_ok, 1)
            if ahead:
                w12_lo(j + 2, par, (s + 2) % RAWS)

        for n in range(2):
            w12_lo(n, n, n)
            x_lo(n, n)
        for blk_ in FIRST_BLOCKS:
            step(*blk_)
        for n, (lo, hi) in enumerate(LOOPS):
            with dve.Fori(lo, hi) as i:
                for blk_ in group(i):
                    step(*blk_)
            if n == 0:
                dve.wait_ge(s4p_ok, ANGLE)
                dve.tensor_scalar(angle[:, :, :], angle[:, :, :], PI_SAFE, -PI_SAFE, ALU.min, ALU.max).then_inc(s4v_ok, 1)
        for blk_ in LAST_BLOCKS:
            step(*blk_, ahead=(blk_[0] + 2 < NB))
        split_lo(1, 3)

        dve.wait_ge(gw_ok, 1)
        tt(gwc[:, :, NE1:2 * NE1], gwraw[:, :, :], f(gwc[:, :, 0:NE1]), ALU.subtract).then_inc(gw_ok, 1)

        def combine(n0, n1):
            for n in range(n0, n1):
                i, k = n // K, n % K
                dve.wait_ge(yg_in[n % YS], 16 * (n // YS + 1))
                if k:
                    wait(dve, comb_ok, n)
                dve.scalar_tensor_tensor(acc[:, i, :], yg[:, n % YS, :], gk[:, k, i:i + 1], acc[:, i, :], ALU.mult,
                                         ALU.add).then_inc(comb_ok, 1)

        shared_hid(2)
        for par in range(2):
            wait(dve, ys_out[par], 16 * ((NB + 1 - par) // 2))
        shared_lo(2)
        combine(0, 8)
        shared_hid(3)
        shared_lo(3)
        dve.wait_ge(comb_ok, 8)
        for i in range(TH):
            add_y(2, i)

        def conv_input(i):
            dve.wait_ge(xt_done, i + 1)
            tt(u_t[:, :, :, BT * i:BT * i + BT].rearrange("p h k b -> p k b h"),
               bank[XT_BANK[i]][:, :].rearrange("p (k b h) -> p k b h", k=KC, b=BT),
               mask[:, 1, :, BT * i:BT * i + BT].unsqueeze(3).broadcast_to([P, KC, BT, C]), ALU.mult).then_inc(u_ok, 1)

        dve.wait_ge(mask_ok, 1)
        combine(8, 16)
        dve.wait_ge(comb_ok, 16)
        conv_input(0)
        conv_input(1)
        for i in range(TH):
            add_y(3, i)
        for i in range(2, NT):
            conv_input(i)

        def y_lo(g):
            dve.wait_ge(yh_ok, g + 1)
            tt(al[:, :, :].rearrange("p k (b h) -> p h k b", h=C)[:, 4 * g:4 * g + 4],
               ycv[:, g % 2, :, :].rearrange("p h (k b) -> p h k b", k=KC),
               f(ah[:, :, :]).rearrange("p k (b h) -> p h k b", h=C)[:, 4 * g:4 * g + 4], ALU.subtract)\
                .then_inc(yl_ok, 1)

        for g in range(C // 4):
            wait(dve, conv_done, 4 * g + 4)
            wait(dve, yh_ok, g - 1)
            wait(dve, yl_ok, g - 1)
            tt(ycv[:, g % 2, :, :], bank[g % 4][:, :].rearrange("p (h n) -> p h n", h=4),
               mask[:, 0, :, :].rearrange("p k b -> p (k b)").unsqueeze(1).broadcast_to([P, 4, P]), ALU.mult)\
                .then_inc(y_ok, 1)
            if g:
                y_lo(g - 1)
            if C // 4 - KC <= g + 1 < C // 4:
                k = g + 1 - (C // 4 - KC)
                dve.wait_ge(uph_ok, k + 1)
                tt(upl[:, k, :], upraw[:, k, :], f(uph[:, k, :]), ALU.subtract).then_inc(upl_ok, 1)
        y_lo(C // 4 - 1)
        dve.wait_ge(lg_done, 2)
        lgv = bank[2][:, 0:NT * 2 * NE1].rearrange("p (i r e) -> p i r e", r=2, e=NE1)
        link(dve.tensor_copy(lg1[:, :, :], lgv[:, :, 1, :]))
        tt(lg1[:, :, :], lgv[:, :, 0, :], lg1[:, :, :], ALU.add).then_inc(top_ok, 1)

        def moments(i):
            dve.wait_ge(rt_done, i + 1)
            link(dve.bn_stats(stats[:, i, :], bank[i % TH][:, :]))
            dve.bn_aggr(mv[:, i, :], stats[:, i, :]).then_inc(var_ok, 1)

        def scales(i):
            dve.wait_ge(std_ok, i + 1)
            link(dve.reciprocal(rstd[:, i:i + 1], std[:, i:i + 1]))
            dve.scalar_tensor_tensor(nmr[:, i:i + 1], mv[:, i, 0:1], -1.0, rstd[:, i:i + 1], ALU.mult, ALU.mult)\
                .then_inc(nmr_ok, 1)

        def finish(i):
            o = osum[:, i % TH, :]
            dve.wait_ge(norm_ok, i + 1)
            if i == 0:
                dve.wait_ge(ln_in, 32)
            link(tt(o, o, gam[:, :], ALU.mult))
            dve.wait_ge(resid_ok, i + 1)
            tt(acc[:, i, :], o, acc[:, i, :], ALU.add).then_inc(fin_ok, 1)

        for q in range(2):
            for j in range(JC):
                v = q * JC + j
                if j == JC - 1:
                    for a in range(LC):
                        dve.wait_ge(lat_done, LC * q + a + 1)
                        dve.wait_ge(rscb_ok, 2)
                        wait(dve, lath_ok, q * LC)
                        tt(latf[:, a, :], bank[6 + a][:, :], rscb[:, q, :], ALU.mult).then_inc(latf_ok, 1)
                dve.wait_ge(rel_ok, v + 1)
                wait(dve, sqh_ok, v - 1)
                wait(dve, sql_ok, v - 1)
                tt(sq[:, v % 2, :], rel[:, v % 2, :], rel[:, v % 2, :], ALU.mult).then_inc(sq_ok, 1)
                if j == JC - 1:
                    for a in range(LC):
                        dve.wait_ge(lath_ok, LC * q + a + 1)
                        wait(dve, rt_done, q * TH)
                        tt(latl[:, a, :], latf[:, a, :], f(lath[:, a, :]), ALU.subtract).then_inc(latl_ok, 1)
                dve.wait_ge(sqh_ok, v + 1)
                wait(dve, dn_done, (v - 1) * TH)
                tt(sql[:, v % 2, :], sq[:, v % 2, :], f(sqh[:, v % 2, :]), ALU.subtract).then_inc(sql_ok, 1)
                if q and j < TH:
                    finish(j)
                if v == 1:
                    dve.wait_ge(top_ok, 1)
                    for i in range(NT):
                        dve.max(top8[:, i, :], lg1[:, i, :]).then_inc(top_ok, 1)
                    dve.wait_ge(top_ok, NT + 1)
                    tt(rsc[:, :], top8[:, :, 0], top8[:, :, 1], ALU.add).then_inc(rsc_ok, 1)
                if v == 2:
                    for a in range(LC):
                        dve.wait_ge(m2h_ok, a + 1)
                        tt(m2l[:, a, :], bank[6 + a][:, :], f(m2h[:, a, :]), ALU.subtract).then_inc(m2l_ok, 1)
            if q == 0:
                moments(0)
                for i in range(TH):
                    if i + 1 < TH:
                        moments(i + 1)
                    scales(i)
            else:
                for i in range(TH, NT):
                    moments(i)
                    scales(i)
                    if i > TH:
                        finish(i - 1)
                finish(NT - 1)

    @block.tensor
    def _(pe):
        pe.wait_ge(warm_ok, 1)
        for _ in range(WARM):
            pe.matmul(bank[7][:, :], warm[:, 0:P], warm[:, :], start=True, stop=True)
        def transpose_mixed(i):
            pe.wait_ge(xst_ok, i + 1)
            wait(pe, al_ok, i - 3)
            for k in range(KC):
                mm = pe.transpose(bank[2 * i % 8][:, k * P:(k + 1) * P], xstage[:, i % 4, k * P:(k + 1) * P], ident[:, :])
            mm.then_inc(mix_done, 1)

        for i in range(NT):
            if i == 2:
                pe.wait_ge(s4b_in, 32)
                pe.wait_ge(s4_in, 64)
                pe.wait_ge(stage_ok, 1)
                for k in range(4):
                    mm = pe.transpose(bank[7][:, k * C:(k + 1) * C], sstage[:, k, :], ident[0:C, 0:C])
                mm.then_inc(tr_done, 1)
            if i == 3:
                pe.wait_ge(spar_ok, 1)
            pe.wait_ge(wbd_ok, BT if i < 2 else 2 * BT)
            pe.wait_ge(x_in[i // 2], 16)
            wait(pe, xst_ok, i - 3)
            pe.matmul(bank[(2 * i + 1) % 8][:, :], wbd[:, i, :], acc[:, i, :], start=True, stop=True)\
                .then_inc(mixr_done, 1)
            if i == 0:
                pe.wait_ge(const_ok, IDENT)
            else:
                transpose_mixed(i - 1)
        transpose_mixed(NT - 1)

        def logits(w, q, dst):
            for k in range(KC):
                for part in (ah, al):
                    mm = pe.matmul(dst, w[:, k, :], part[:, k, q * HALF:(q + 1) * HALF],
                                   start=(k == 0 and part is ah), stop=(k == KC - 1 and part is al))
            return mm

        pe.wait_ge(rw_ok, 2)
        for q in range(2):
            wait(pe, ah_ok, (q + 1) * TH)
            wait(pe, al_ok, (q + 1) * TH)
            if q == 0:
                pe.wait_ge(al_ok, TH + 1)
            pe.wait_ge(xst_ok, NT)
            logits(rwc, q, bank[q][0:2 * E, :]).then_inc(lgt_done, 1)
        pe.wait_ge(bias_in, 64)
        for k in range(2):
            mm = pe.transpose(bank[3][:, k * G:(k + 1) * G], bstage[:, k, :], ident[0:G, 0:G])
        mm.then_inc(tr_done, 1)
        pe.wait_ge(lgt_ok, 2)
        for i in range(NT):
            mm = pe.transpose(bank[2][:, i * 2 * E:(i + 1) * 2 * E], ltr[:, i // TH, i % TH * P:(i % TH + 1) * P],
                              ident[0:2 * E, 0:2 * E])
        mm.then_inc(lg_done, 1)

        def y_products(u):
            q = u % 2
            pe.wait_ge(hidh_ok, u + 1)
            pe.wait_ge(hidl_ok, u + 1)
            for i in range(TH):
                s = slice(i * P, (i + 1) * P)
                wait(pe, y_added, u * 4 + i - 3)
                if u >= 2:
                    t = q * HALF + i * P
                    pe.matmul(bank[i][:, :], gt[:, t:t + P], b3m[:, :], start=True, stop=False)
                split3(pe, bank[i][:, :], lambda k: (hidh[:, q, s], hidl[:, q, s]),
                       lambda k: (whi[:, 1, W3], wlo[:, 1, W3]), 1, start=(u < 2)).then_inc(y_done, 1)

        def shared_products(u):
            q = u % 2
            pe.wait_ge(swh_ok, u // 2 + 1)
            pe.wait_ge(swl_ok, u // 2 + 1)
            tok = slice(q * HALF, (q + 1) * HALF)
            for off, ready, sem_done, dst in ((0, silu_ok, a_done, 4), (KC, hid_ok, c_done, 6)):
                wait(pe, ready, u - 1)
                split3(pe, bank[dst + q][:, :],
                       lambda k: (whi[:, 1, (off + k) * P:(off + k + 1) * P],
                                  wlo[:, 1, (off + k) * P:(off + k + 1) * P]),
                       lambda k: (ah[:, k, tok], al[:, k, tok]), KC).then_inc(sem_done, 1)

        pe.wait_ge(xst_ok, NT)
        shared_products(0)
        pe.wait_ge(const_ok, TRI)
        pe.wait_ge(msk_ok, 1)
        wm = w2t[:, :, :].rearrange("p i e -> p (i e)")
        pe.matmul(bank[2][:, 0:NT * E], tri[:, :], wm, start=True, stop=True)
        pe.matmul(bank[2][:, NT * E:2 * NT * E], ones[:, :], wm, start=True, stop=True).then_inc(rank_done, 1)
        shared_products(1)
        for n in range(K * NT):
            pe.wait_ge(hot_ok, K + n // NT + 1)
            mm = pe.matmul(bank[3][:, 0:NSLOT], hotp[:, n, :], hotb[:, n, :], start=(n == 0), stop=(n == K * NT - 1))
        mm.then_inc(tok_done, 1)
        pe.wait_ge(rank_ok, 1)
        pe.wait_ge(b12_ok, 1)
        pe.wait_ge(tok_ok, 1)
        for u in range(2):
            y_products(u)

        def transpose_x(n, par, s, ms):
            pe.wait_ge(xg_in[s], ms * 16 + 16)
            wait(pe, bxl_ok, n - 1)
            for k in range(KC):
                mm = pe.transpose(bank[par][:, k * P:(k + 1) * P], xg[:, s, k * P:(k + 1) * P], ident[:, :])
            mm.then_inc(bx_done, 1)

        def block_y(n, par):
            pe.wait_ge(w3l_ok, n + 1)
            pe.wait_ge(bhl_ok, n + 1)
            wait(pe, yout_ok, n - 1)
            split3(pe, bank[6 + par][:, :], lambda k: (bhh[:, par, :], bhl[:, par, :]),
                   lambda k: (whi[:, par, W3], wlo[:, par, W3]), 1).then_inc(by_done, 1)

        def step(j, par, m, s, ms, ahead=True):
            pe.wait_ge(bxl_ok, j + 1)
            pe.wait_ge(w12l_ok, j + 1)
            wait(pe, bhl_ok, j - 1)
            h = bank[2 + par][:, 0:2 * P]
            for part in range(2):
                pe.matmul(h, onesr[:, :], brow(s)[:, part, :], start=(part == 0), stop=False)
            wh = whi[:, par, W12].rearrange("p (w k m) -> p k w m", w=2, k=KC)
            wl = wlo[:, par, W12].rearrange("p (w k m) -> p k w m", w=2, k=KC)
            hv = h.rearrange("p (w m) -> p w m", w=2)
            for k in range(KC):
                pe.matmul(hv, xth[:, par, k, :], wh[:, k], start=False, stop=False)
                pe.matmul(hv, xth[:, par, k, :], wl[:, k], start=False, stop=False)
                mm = pe.matmul(hv, xtl[:, par, k, :], wh[:, k], start=False, stop=(k == KC - 1))
            mm.then_inc(bh_done, 1)
            if not (isinstance(j, int) and j == 0):
                block_y(j - 1, 1 - par)
            if ahead:
                transpose_x(j + 2, par, (s + 2) % RAWS, ms + (s + 2) // RAWS)
            pe.wait_ge(bhid_ok, j + 1)
            pe.transpose(bank[2 + par][:, 2 * P:3 * P], bhid[:, par, :], ident[:, :]).then_inc(bt_done, 1)

        for n in range(2):
            pe.wait_ge(y_added, 4 + n + 1)
            transpose_x(n, n, n, 0)
        pe.wait_ge(y_added, 8)
        for blk_ in FIRST_BLOCKS:
            step(*blk_)
        for n, (lo, hi) in enumerate(LOOPS):
            with pe.Fori(lo, hi) as i:
                for blk_ in group(i):
                    step(*blk_)
            if n == 2:
                pe.wait_ge(l1_in, 16 * 7)
                for m in range(LC):
                    for l in range(LC):
                        mm = pe.transpose(bank[4][:, m * LAT + l * P:m * LAT + (l + 1) * P],
                                          ewraw[:, l, m * P:(m + 1) * P], ident[:, :])
                mm.then_inc(tr_done, 1)
                pe.wait_ge(lhs_ok, 1)
                for j in (1, 0):
                    if j == 0:
                        pe.wait_ge(ewt_ok, 1)
                    for h in range(16 * j, 16 * j + 16):
                        c = (h % 16) * LJ
                        mm = pe.matmul(bank[4 + j][0:LI, c:c + LJ], lhs_k[:, h, :], term[:, h, 2 * LI:2 * LI + LJ],
                                       start=True, stop=True)
                    mm.then_inc(k_done, 1)
        for blk_ in LAST_BLOCKS:
            step(*blk_, ahead=(blk_[0] + 2 < NB))
        block_y(NB - 1, (NB - 1) % 2)

        pe.wait_ge(gates_ok, 2)
        pe.wait_ge(kout_ok, 2)
        for j in range(2):
            for i in range(TH):
                mm = pe.transpose(bank[4 + j][0:G, i * P:(i + 1) * P], gates[:, :, j * TH + i], ident[:, :])
            mm.then_inc(gt_done, 1)
        pe.wait_ge(gt_ok, 2)
        pe.wait_ge(yout_ok, NB)
        shared_products(2)
        shared_products(3)
        y_products(2)
        y_products(3)
        pe.wait_ge(silu_ok, 4)
        pe.wait_ge(hid_ok, 4)
        for i in range(NT):
            pe.wait_ge(arev_ok, i + 1)
            if i < TH:
                wait(pe, u_ok, i - 1)
            elif i < TH + 2:
                pe.wait_ge(y_added, 16)
            else:
                pe.wait_ge(u_ok, i - 3)
            for k in range(KC):
                mm = pe.transpose(bank[XT_BANK[i]][:, k * P:(k + 1) * P], arev[:, i % 2, (KC - 1 - k) * P:(KC - k) * P],
                                  ident[:, :])
            mm.then_inc(xt_done, 1)
            if i in M2_AFTER:
                a, m = divmod(M2_AFTER.index(i), LC)
                mm = pe.matmul(bank[6 + a][:, :], ewt[:, m, a * P:(a + 1) * P], fc2raw[:, m, :],
                               start=(m == 0), stop=(m == LC - 1))
                if m == LC - 1:
                    mm.then_inc(m2_done, 1)
        pe.wait_ge(u_ok, NT)
        for h in range(C):
            if h < TS and h % (TS // 3) == 0:
                pe.wait_ge(toep_in[h // (TS // 3)], 64 if h == 0 else 16)
            if h == TS:
                pe.wait_ge(toep_in[3], 16)
            if h % 4 == 0:
                wait(pe, y_ok, h // 4 - 3)
            for d in range(KC):
                c = (h % 4) * P
                mm = pe.matmul(bank[h // 4 % 4][:, c + d * B:c + P], toep[:, h % TS, d * P:(d + 1) * P],
                               u_t[:, h, 0:KC - d, :].rearrange("p k b -> p (k b)"), start=(d == 0), stop=(d == KC - 1))
            mm.then_inc(conv_done, 1)
        pe.wait_ge(yh_ok, C // 4)
        pe.wait_ge(yl_ok, C // 4)
        pe.wait_ge(gw_ok, 2)
        for q in range(2):
            logits(gwc, q, bank[q][0:2 * NE1, :]).then_inc(lgt_done, 1)

        def down_tile(v, i):
            q, j = v // JC, v % JC
            s = slice(i * P, (i + 1) * P)
            pe.wait_ge(sqh_ok, v + 1)
            pe.wait_ge(sql_ok, v + 1)
            pe.wait_ge(dnh_ok, j + 1)
            pe.wait_ge(dnl_ok, j + 1)
            if j == 0:
                wait(pe, norm_ok, (q - 1) * TH + i + 1)
            split3(pe, bank[i][:, :], lambda k: (sqh[:, v % 2, s], sql[:, v % 2, s]),
                   lambda k: (dnh[:, j, :], dnl[:, j, :]), 1, start=(j == 0), stop=False).then_inc(dn_done, 1)

        def latent(q):
            tok = slice(q * HALF, (q + 1) * HALF)
            pe.wait_ge(fch_ok, 1)
            pe.wait_ge(fcl_ok, 1)
            pe.wait_ge(m2l_ok, LC)
            wait(pe, latf_ok, q * LC)
            if q == 0:
                pe.wait_ge(rsc_ok, 1)
                for i in range(NT):
                    mm = pe.matmul(bank[6 + i // TH][:, i % TH * P:(i % TH + 1) * P],
                                   rsc[:, i:i + 1].broadcast_to([P, P]), ident[:, :], start=True, stop=True)
                mm.then_inc(rscb_done, 1)
                pe.wait_ge(rscb_ok, 2)
            for a in range(LC):
                s = slice(a * P, (a + 1) * P)
                split3(pe, bank[6 + a][:, :], lambda k: (fch[:, k, s], fcl[:, k, s]),
                       lambda k: (ah[:, k, tok], al[:, k, tok]), KC).then_inc(lat_done, 1)

        pe.wait_ge(uph_ok, KC)
        pe.wait_ge(upl_ok, KC)
        for q in range(2):
            tok = slice(q * HALF, (q + 1) * HALF)
            for j in range(JC):
                v = q * JC + j
                s = slice(j * P, (j + 1) * P)
                wait(pe, rel_ok, v - 1)
                split3(pe, bank[4 + v % 2][:, :], lambda k: (uph[:, k, s], upl[:, k, s]),
                       lambda k: (ah[:, k, tok], al[:, k, tok]), KC).then_inc(up_done, 1)
                if v == 0:
                    pe.wait_ge(lgt_ok, 4)
                    for i in range(NT):
                        mm = pe.transpose(bank[2][:, i * 2 * NE1:(i + 1) * 2 * NE1],
                                          ltg[:, i // TH, i % TH * P:(i % TH + 1) * P], ident[0:2 * NE1, 0:2 * NE1])
                    mm.then_inc(lg_done, 1)
                if j:
                    if v == 1:
                        pe.wait_ge(top_ok, 1)
                    for i in range(TH):
                        down_tile(v - 1, i)
                if j == JC - 2:
                    latent(q)
            pe.wait_ge(lath_ok, LC * (q + 1))
            pe.wait_ge(latl_ok, LC * (q + 1))
            for i in range(TH):
                down_tile(q * JC + JC - 1, i)
                s = slice(i * P, (i + 1) * P)
                split3(pe, bank[i][:, :], lambda a: (lath[:, a, s], latl[:, a, s]),
                       lambda a: (m2h[:, a, :], m2l[:, a, :]), LC, start=False).then_inc(rt_done, 1)

    ctx.close()


_INS = ["x", "itok_B_0_15", "itok_B_8_3872", "L0_cond_weights", "L0_ffn_router_w", "L0_ffn_router_b",
        "L0_ffn_router_bias", "L0_ffn_ew1", "L0_ffn_eb1", "L0_ffn_ew2", "L0_ffn_eb2", "L0_ffn_ew3", "L0_ffn_eb3",
        "L0_ffn_sw1", "L0_ffn_sb1", "L0_ffn_sw2", "L0_ffn_sb2", "L0_ffn_sw3", "L0_ffn_sb3", "L1_cond_log_dt",
        "L1_cond_C", "L1_cond_log_A_real", "L1_cond_A_imag", "L1_cond_D", "L1_ffn_gate_w", "L1_ffn_up_w",
        "L1_ffn_down_w", "L1_ffn_fc1_w", "L1_ffn_fc2_w", "L1_ffn_expert_w", "L1_ffn_ln_gamma", "L1_ffn_ln_beta"]


def kernel(**inputs):
    import concourse.bacc as bacc
    from concourse.bass_utils import run_bass_kernel_spmd

    nc = bacc.Bacc("TRN2", target_bir_lowering=False, num_devices=1)
    arrays, args = {}, []
    for name in _INS:
        a = np.ascontiguousarray(inputs[name])
        arrays[f"in_{name}"] = a
        args.append(nc.dram_tensor(f"in_{name}", a.shape, mybir.dt.from_np(a.dtype), kind="ExternalInput").ap())
    res = nc.dram_tensor("out_0", inputs["x"].shape, F32, kind="ExternalOutput").ap()
    adaln_ffn_program(nc, *args, res)
    r = run_bass_kernel_spmd(nc, [arrays], core_ids=[0])
    return r.results[0]["out_0"]
```
